# Optimizing a Trainium2 kernel written in Bass

```python
import numpy as np
import jax
import jax.numpy as jnp

def _softmax(x, axis=-1):
    return jax.nn.softmax(x, axis=axis)

def _gelu(x):
    return jax.nn.gelu(x, approximate=True)

def _silu(x):
    return jax.nn.silu(x)

def _sigmoid(x):
    return jax.nn.sigmoid(x)

def _layernorm(x, axis=-1, eps=1e-05):
    m = jnp.mean(x, axis=axis, keepdims=True)
    v = jnp.var(x, axis=axis, keepdims=True)
    return (x - m) / jnp.sqrt(v + eps)

def _scatter_add(tgt, idx, src, axis=0):
    return tgt.at[idx].add(src)

def _segment_sum(src, seg, n):
    return jax.ops.segment_sum(src, seg, n)
kernel_name = 'mk_prb_d1_jaxref_r8_12c2d6'

def setup_inputs(seed: int=0):
    np.random.seed(seed)
    _w = jnp.asarray

    def _L0_attn_setup():
        import jax, jax.numpy as jnp
        import numpy as np
        from jax import lax
        H, KVH, D, CHUNK = (32, 8, 128, 128)
        ROPE_THETA = 10000.0
        RMS_EPS = 1e-05

        def _rope_tables(L):
            inv_freq = 1.0 / ROPE_THETA ** (jnp.arange(0, D, 2, dtype=jnp.float32) / D)
            ang = jnp.arange(L, dtype=jnp.float32)[:, None] * inv_freq
            cos = jnp.concatenate([jnp.cos(ang), jnp.cos(ang)], axis=-1)[:, None, :]
            sin = jnp.concatenate([jnp.sin(ang), jnp.sin(ang)], axis=-1)[:, None, :]
            return (cos, sin)

        def _apply_rope(x, cos, sin):
            half = D // 2
            rot = jnp.concatenate([-x[..., half:], x[..., :half]], axis=-1)
            return x * cos + rot * sin
        key = jax.random.key(seed)
        ks = jax.random.split(key, 10)
        B, L, HID = (1, 512, 512)
        s = lambda fan: 1.0 / np.sqrt(fan)
        return {'hidden_states': jax.random.normal(ks[0], (B, L, HID), jnp.float32), 'Wq': jax.random.normal(ks[1], (H * D, HID), jnp.float32) * s(HID), 'Wk': jax.random.normal(ks[2], (KVH * D, HID), jnp.float32) * s(HID), 'Wv': jax.random.normal(ks[3], (KVH * D, HID), jnp.float32) * s(HID), 'Wo': jax.random.normal(ks[4], (HID, H * D), jnp.float32) * s(H * D), 'Wg': jax.random.normal(ks[5], (H * D, HID), jnp.float32) * (s(HID) * 2 ** (-2.5)), 'Win': jax.random.normal(ks[6], (H, HID), jnp.float32) * s(HID), 'dt_bias': jnp.zeros((H,), jnp.float32), 'A_log_bias': jnp.log(jax.random.uniform(ks[7], (H,), jnp.float32, 1.0, 16.0)), 'gnorm_w': jnp.ones((D,), jnp.float32)}
    _L0_attn_in = _L0_attn_setup()

    def _L0_ffn_setup():
        import jax, jax.numpy as jnp
        import numpy as np
        DIM = 512
        INTER = 128
        E = 16
        GROUPS = 4
        LIM = 2
        K = 2
        SHARED_INTER = 2 * INTER
        SCALE = 1.0
        key = jax.random.key(seed)
        ks = jax.random.split(key, 16)

        def n(k, shape, s=0.02):
            return jax.random.normal(k, shape, jnp.float32) * s
        return {'x': jax.random.normal(ks[0], (1, 256, DIM), jnp.float32), 'router_w': n(ks[1], (DIM, E)), 'router_b': n(ks[2], (E,)), 'router_bias': n(ks[3], (E,), 1.0), 'ew1': n(ks[4], (E, DIM, INTER)), 'eb1': n(ks[5], (E, INTER)), 'ew2': n(ks[6], (E, DIM, INTER)), 'eb2': n(ks[7], (E, INTER)), 'ew3': n(ks[8], (E, INTER, DIM)), 'eb3': n(ks[9], (E, DIM)), 'sw1': n(ks[10], (DIM, SHARED_INTER)), 'sb1': n(ks[11], (SHARED_INTER,)), 'sw2': n(ks[12], (DIM, SHARED_INTER)), 'sb2': n(ks[13], (SHARED_INTER,)), 'sw3': n(ks[14], (SHARED_INTER, DIM)), 'sb3': n(ks[15], (DIM,))}
    _L0_ffn_in = _L0_ffn_setup()
    _d = {'L0_attn_hidden_states': _L0_attn_in['hidden_states'], 'L0_attn_Wq': _L0_attn_in['Wq'], 'L0_attn_Wk': _L0_attn_in['Wk'], 'L0_attn_Wv': _L0_attn_in['Wv'], 'L0_attn_Wo': _L0_attn_in['Wo'], 'L0_attn_Wg': _L0_attn_in['Wg'], 'L0_attn_Win': _L0_attn_in['Win'], 'L0_attn_dt_bias': _L0_attn_in['dt_bias'], 'L0_attn_A_log_bias': _L0_attn_in['A_log_bias'], 'L0_attn_gnorm_w': _L0_attn_in['gnorm_w'], 'L0_ffn_router_w': _L0_ffn_in['router_w'], 'L0_ffn_router_b': _L0_ffn_in['router_b'], 'L0_ffn_router_bias': _L0_ffn_in['router_bias'], 'L0_ffn_ew1': _L0_ffn_in['ew1'], 'L0_ffn_eb1': _L0_ffn_in['eb1'], 'L0_ffn_ew2': _L0_ffn_in['ew2'], 'L0_ffn_eb2': _L0_ffn_in['eb2'], 'L0_ffn_ew3': _L0_ffn_in['ew3'], 'L0_ffn_eb3': _L0_ffn_in['eb3'], 'L0_ffn_sw1': _L0_ffn_in['sw1'], 'L0_ffn_sb1': _L0_ffn_in['sb1'], 'L0_ffn_sw2': _L0_ffn_in['sw2'], 'L0_ffn_sb2': _L0_ffn_in['sb2'], 'L0_ffn_sw3': _L0_ffn_in['sw3'], 'L0_ffn_sb3': _L0_ffn_in['sb3']}
    _x0 = _d['L0_attn_hidden_states']
    _d['L0_attn_hidden_states'] = jax.random.normal(jax.random.fold_in(jax.random.key(seed), 1), (4, 512, 512), dtype=_x0.dtype)
    del _x0
    return _d

def reference(L0_attn_hidden_states, L0_attn_Wq, L0_attn_Wk, L0_attn_Wv, L0_attn_Wo, L0_attn_Wg, L0_attn_Win, L0_attn_dt_bias, L0_attn_A_log_bias, L0_attn_gnorm_w, L0_ffn_router_w, L0_ffn_router_b, L0_ffn_router_bias, L0_ffn_ew1, L0_ffn_eb1, L0_ffn_ew2, L0_ffn_eb2, L0_ffn_ew3, L0_ffn_eb3, L0_ffn_sw1, L0_ffn_sb1, L0_ffn_sw2, L0_ffn_sb2, L0_ffn_sw3, L0_ffn_sb3):

    def _L0_attn_ref(hidden_states, Wq, Wk, Wv, Wo, Wg, Win, dt_bias, A_log_bias, gnorm_w):
        import jax, jax.numpy as jnp
        import numpy as np
        from jax import lax
        H, KVH, D, CHUNK = (32, 8, 128, 128)
        ROPE_THETA = 10000.0
        RMS_EPS = 1e-05

        def _rope_tables(L):
            inv_freq = 1.0 / ROPE_THETA ** (jnp.arange(0, D, 2, dtype=jnp.float32) / D)
            ang = jnp.arange(L, dtype=jnp.float32)[:, None] * inv_freq
            cos = jnp.concatenate([jnp.cos(ang), jnp.cos(ang)], axis=-1)[:, None, :]
            sin = jnp.concatenate([jnp.sin(ang), jnp.sin(ang)], axis=-1)[:, None, :]
            return (cos, sin)

        def _apply_rope(x, cos, sin):
            half = D // 2
            rot = jnp.concatenate([-x[..., half:], x[..., :half]], axis=-1)
            return x * cos + rot * sin
        B, L, HID = hidden_states.shape
        NC = L // CHUNK
        q = (hidden_states @ Wq.T).reshape(B, L, H, D)
        k = (hidden_states @ Wk.T).reshape(B, L, KVH, D)
        v = (hidden_states @ Wv.T).reshape(B, L, KVH, D)
        cos, sin = _rope_tables(L)
        q = _apply_rope(q, cos, sin)
        k = _apply_rope(k, cos, sin)
        k = jnp.repeat(k, H // KVH, axis=2)
        v = jnp.repeat(v, H // KVH, axis=2)
        dt = jax.nn.softplus(hidden_states @ Win.T + dt_bias)
        A = -jnp.exp(A_log_bias)
        g = dt * A

        def chunked(t):
            return t.transpose(0, 2, 1, 3).reshape(B, H, NC, CHUNK, D)
        qc, kc = (chunked(q), chunked(k))
        xc = chunked(v * dt[..., None])
        gc = g.transpose(0, 2, 1).reshape(B, H, NC, CHUNK)
        G = jnp.cumsum(gc, axis=-1)
        scores = jnp.einsum('bhnid,bhnjd->bhnij', qc, kc)
        idx = jnp.arange(CHUNK)
        causal = idx[:, None] >= idx[None, :]
        decay = jnp.where(causal, jnp.exp(G[..., :, None] - G[..., None, :]), 0.0)
        y_intra = jnp.einsum('bhnij,bhnjd->bhnid', scores * decay, xc)
        Glast = G[..., -1:]
        k_dec = kc * jnp.exp(Glast - G)[..., None]
        cstates = jnp.einsum('bhnjd,bhnje->bhnde', k_dec, xc)
        chunk_decay = jnp.exp(G[..., -1])

        def step(state, inp):
            dec, cs = inp
            return (state * dec + cs, state)
        init = jnp.zeros((B, H, D, D), hidden_states.dtype)
        _, prev = lax.scan(step, init, (chunk_decay.transpose(2, 0, 1)[..., None, None], cstates.transpose(2, 0, 1, 3, 4)))
        prev = prev.transpose(1, 2, 0, 3, 4)
        y_inter = jnp.einsum('bhnid,bhnde->bhnie', qc * jnp.exp(G)[..., None], prev)
        y = (y_intra + y_inter).reshape(B, H, L, D).transpose(0, 2, 1, 3)
        rms = jnp.sqrt(jnp.mean(jnp.square(y), axis=-1, keepdims=True) + RMS_EPS)
        y = y / rms * gnorm_w
        gate = (hidden_states @ Wg.T).reshape(B, L, H, D)
        y = y * (gate * jax.nn.sigmoid(gate))
        return y.reshape(B, L, H * D) @ Wo.T

    def _L0_ffn_ref(x, router_w, router_b, router_bias, ew1, eb1, ew2, eb2, ew3, eb3, sw1, sb1, sw2, sb2, sw3, sb3):
        import jax, jax.numpy as jnp
        import numpy as np
        DIM = 512
        INTER = 128
        E = 16
        GROUPS = 4
        LIM = 2
        K = 2
        SHARED_INTER = 2 * INTER
        SCALE = 1.0
        shape = x.shape
        xt = x.reshape(-1, DIM)
        T = xt.shape[0]
        logits = xt @ router_w + router_b
        scores = jax.nn.softmax(logits.astype(jnp.float32), axis=-1) + router_bias
        g = scores.reshape(T, GROUPS, E // GROUPS)
        _, gidx = jax.lax.top_k(g.max(axis=-1), LIM)
        keep = jnp.zeros((T, GROUPS), bool).at[jnp.arange(T)[:, None], gidx].set(True)
        masked = jnp.where(keep[:, :, None], g, -jnp.inf).reshape(T, E)
        _, idx = jax.lax.top_k(masked, K)
        vals = (jnp.take_along_axis(scores, idx, axis=1) * SCALE).astype(x.dtype)
        gate = jnp.zeros((T, E), x.dtype).at[jnp.arange(T)[:, None], idx].add(vals)

        def step(y, p):
            w1, b1, w2, b2, w3, b3, ge = p
            h = jax.nn.silu(xt @ w1 + b1) * (xt @ w2 + b2)
            return (y + ge[:, None] * (h @ w3 + b3), None)
        y, _ = jax.lax.scan(step, jnp.zeros_like(xt), (ew1, eb1, ew2, eb2, ew3, eb3, gate.T))
        z = jax.nn.silu(xt @ sw1 + sb1) * (xt @ sw2 + sb2) @ sw3 + sb3
        return (y + z).reshape(shape)
    x = L0_attn_hidden_states
    xn = _layernorm(x, axis=-1)
    x = x + _L0_attn_ref(xn, L0_attn_Wq, L0_attn_Wk, L0_attn_Wv, L0_attn_Wo, L0_attn_Wg, L0_attn_Win, L0_attn_dt_bias, L0_attn_A_log_bias, L0_attn_gnorm_w) + _L0_ffn_ref(xn, L0_ffn_router_w, L0_ffn_router_b, L0_ffn_router_bias, L0_ffn_ew1, L0_ffn_eb1, L0_ffn_ew2, L0_ffn_eb2, L0_ffn_ew3, L0_ffn_eb3, L0_ffn_sw1, L0_ffn_sb1, L0_ffn_sw2, L0_ffn_sb2, L0_ffn_sw3, L0_ffn_sb3)
    return x

_drawn_inputs = setup_inputs


def setup_inputs(seed=0):
    import zlib

    import numpy as np

    out = dict(_drawn_inputs(seed))
    spreads = {'L0_attn_dt_bias': (0.0, 2.0), 'L0_attn_gnorm_w': (1.0, 0.6)}
    factors = {'L0_ffn_router_w': 8.0,
     'L0_ffn_router_b': 167.384,
     'L0_ffn_eb1': 8.0,
     'L0_ffn_eb2': 8.0,
     'L0_ffn_sb1': 34.311,
     'L0_ffn_sb2': 33.29,
     'L0_ffn_sb3': 2.869}
    for name, (base, spread) in spreads.items():
        noise = np.random.default_rng([zlib.crc32(name.encode()), seed]).standard_normal(out[name].shape)
        drawn = base * np.exp(spread * noise) if base else spread * noise
        out[name] = jnp.asarray(drawn.astype(out[name].dtype))
    for name, factor in factors.items():
        out[name] = (out[name] * factor).astype(out[name].dtype)
    return out
```

```python
from contextlib import ExitStack

import numpy as np

import concourse.bass as bass
from concourse import mybir

F32 = mybir.dt.float32
F32R = mybir.dt.float32r
ALU = mybir.AluOpType
ACT = mybir.ActivationFunctionType
AX = mybir.AxisListType

P = 128
HID = 512
KC = HID // P
H, KV, D = 32, 8, 128
HG = H // KV
B, L = 4, 512
NCH = L // P
HALVES = 2
ROWS = B // HALVES
NT = ROWS * NCH
TOK = NT * P
E, GROUPS = 16, 4
EG = E // GROUPS
SLICES = E + 2
RMS_EPS = 1e-5
LN_EPS = 1e-5
MASKED = -1e30
LW = H + E

STEPS = KV * ROWS
ATT_PIECES = 6 + 14 * KV
FFN_PIECES = 4 * (SLICES + 1)
HALF_PIECES = ATT_PIECES + FFN_PIECES
PW = 3 * 512 // 4
BLOCKS = ROWS * SLICES
CONSTS = 16
CONST_DMAS = 9


def build(nc, x, wq, wg, wkv, wo, wlog, dtb, alog, gnw, rb, rbias, w123, b1, b2, b3, cos, sin, gdram, out):
    ctx = ExitStack()
    with ctx:
        def sb(name, shape, dt=F32):
            return ctx.enter_context(nc.sbuf_tensor(name, shape, dt))

        def pb(name):
            return ctx.enter_context(nc.psum_tensor(name, [P, 512], F32))

        xnh = sb("xnh", [P, KC, TOK], F32R)
        xnl = sb("xnl", [P, KC, TOK], F32R)
        acc = sb("acc", [P, NT, HID])
        coef = sb("coef", [P, 4, NT, H])
        negG = coef[:, 0]
        dt = coef[:, 1]
        wdec = coef[:, 2]
        cdec = coef[:, 3]
        hcoef = sb("hcoef", [P, ROWS, 4, NCH, HG])
        fb1 = sb("fb1", [P, 2])
        gate18 = sb("gate18", [P, NT, SLICES + 1])
        wqh = sb("wqh", [P, KC, 512], F32R)
        wql = sb("wql", [P, KC, 512], F32R)
        wgh = sb("wgh", [P, KC, 512], F32R)
        wgl = sb("wgl", [P, KC, 512], F32R)
        woh = sb("woh", [P, HG, 512], F32R)
        wol = sb("wol", [P, HG, 512], F32R)
        wkvh = sb("wkvh", [P, KC, 256], F32R)
        wkvl = sb("wkvl", [P, KC, 256], F32R)
        stage = sb("stage", [P, 2, 512])
        qh = sb("qh", [P, HG, 512], F32R)
        ql = sb("ql", [P, HG, 512], F32R)
        kh = sb("kh", [P, 512], F32R)
        kl = sb("kl", [P, 512], F32R)
        knh = sb("knh", [P, 3, P], F32R)
        knl = sb("knl", [P, 3, P], F32R)
        vh = sb("vh", [P, 512], F32R)
        vl = sb("vl", [P, 512], F32R)
        vf = sb("vf", [P, 512])
        t1 = sb("t1", [P, 512])
        t2 = sb("t2", [P, 2, 512])
        y2 = sb("y2", [P, 512])
        gate = sb("gate", [P, HG, 512])
        yb = sb("yb", [P, NCH, 512])
        rs = sb("rs", [P, NCH, 512])
        zh = sb("zh", [P, 512], F32R)
        zl = sb("zl", [P, 512], F32R)
        gbc = sb("gbc", [P, 2, 512])
        gm = sb("gm", [P, 2, 512])
        wfh = sb("wfh", [P, 512], F32R)
        wfl = sb("wfl", [P, 512], F32R)
        st = sb("st", [P, 512])
        sth = sb("sth", [P, 512], F32R)
        stl = sb("stl", [P, 512], F32R)
        vwh = sb("vwh", [P, 512], F32R)
        vwl = sb("vwl", [P, 512], F32R)
        cosb = sb("cosb", [P, 512])
        sinb = sb("sinb", [P, 512])
        ones = sb("ones", [P, P])
        ident = sb("ident", [P, P])
        upper = sb("upper", [P, P])
        amask = sb("amask", [P, P])
        before = sb("before", [P, E, E])
        dtbb = sb("dtbb", [P, H])
        nA = sb("nA", [P, H])
        rbb = sb("rbb", [P, E])
        rbiasb = sb("rbiasb", [P, E])
        gn = sb("gn", [P, 1])
        b1t = sb("b1t", [P, SLICES])
        b2t = sb("b2t", [P, SLICES])
        rstd = sb("rstd", [P, NT])
        lneps = sb("lneps", [P, 1])
        rmseps = sb("rmseps", [P, 1])
        one = sb("one", [P, 1])

        gflat = gate[:].rearrange("p a b -> p (a b)")
        rflat = rs[:].rearrange("p a b -> p (a b)")
        yflat = yb[:].rearrange("p a b -> p (a b)")
        gmflat = gm[:].rearrange("p a b -> p (a b)")
        wgfh = wgh[:].rearrange("p a b -> p (a b)")
        wgfl = wgl[:].rearrange("p a b -> p (a b)")
        wqfh = wqh[:].rearrange("p a b -> p (a b)")
        wqfl = wql[:].rearrange("p a b -> p (a b)")
        wlh = wgfh[:, 0:KC * LW].rearrange("p (k n) -> p k n", k=KC)
        wll = wgfl[:, 0:KC * LW].rearrange("p (k n) -> p k n", k=KC)
        NH8 = NT * H
        lg = gflat[:, 0:NT * LW].rearrange("p (t n) -> p t n", t=NT)

        def small(i):
            o = NT * LW + i * NH8
            return gflat[:, o:o + NH8].rearrange("p (t n) -> p t n", t=NT)

        zz, ee, uu, ll, dd, gg = [small(i) for i in range(6)]
        gcum = t1[:, 0:NH8]
        b3t = vf[0:E + 1, :]
        bst = st[:, 0:6 * NT].rearrange("p (t n) -> p t n", t=NT)
        mv = st[:, 6 * NT:8 * NT].rearrange("p (t n) -> p t n", t=NT)
        wlraw = rflat[:, 0:KC * LW].rearrange("p (k n) -> p k n", k=KC)

        def route(o, n):
            return rflat[:, KC * LW + o:KC * LW + o + NT * n].rearrange("p (t n) -> p t n", t=NT)

        sm, sc_, mk, rk = route(0, E), route(128, E), route(256, E), route(384, E)
        gmx, grk, keep = route(512, GROUPS), route(544, GROUPS), route(576, GROUPS)
        mx1, sum1, rcp1 = route(608, 1), route(616, 1), route(624, 1)
        gT = gmflat[:, 0:2 * P].rearrange("p (a b) -> p a b", a=2)
        gateT = gmflat[0:E + 1, 2 * P:3 * P]

        PJ = [pb("PJ0"), pb("PJ1")]
        SC, TR, YI, YE, CS, OU = [pb(n) for n in ("SC", "TR", "YI", "YE", "CS", "OU")]

        STEP_N = {}

        def step_sem(name, n):
            s_ = ctx.enter_context(nc.semaphore(name))
            STEP_N[name] = (s_, n)
            return s_

        def sem(name):
            return ctx.enter_context(nc.semaphore(name))

        per_step = dict(
            proj=10, tr=2, score=4, cstate=3, yinter=3, yintra=4, ssq=4, oproj=4,
            vraw=1, ropehi=5, vhi=1, knhi=1, dec=4, expg=3, vwhi=3, whi=4, sthi=3, tanh=4, ysq=4, ssqc=4,
            rsln=1, rms=1, zhi=4,
            coef=1, roperd=5, rope=5, knlo=1, wsc=4, wlo=4, vwlo=3, stt=3, stlo=3, yt=3, y=4, gated=4, u=4, z=4, accd=4,
            ropelo=5, vlo=1, gmask=4, zlo=4,
        )
        LAGGED = {"oproj", "rsln", "rms", "zhi", "z", "accd", "zlo"}
        S = {k: sem("s_" + k) for k in per_step}

        const_in = sem("const_in")
        const_made = sem("const_made")
        passed = sem("passed")
        phase = sem("phase")
        x_in = [sem("x_in0"), sem("x_in1")]
        out_done = sem("out_done")
        wl_in = sem("wl_in")
        stg = [sem("stg0"), sem("stg1")]
        wscaled = sem("wscaled")
        wsplit_hi = sem("wsplit_hi")
        wsplit_lo = sem("wsplit_lo")
        gb_in = [sem("gb_in0"), sem("gb_in1")]
        g_out = sem("g_out")
        dseq = sem("dve_chain")
        aseq = sem("act_chain")
        ln_stats = sem("ln_stats")
        ln_std = sem("ln_std")
        xt_made = sem("xt_made")
        xt_tr = sem("xt_tr")
        xt_hi = sem("xt_hi")
        xt_lo = sem("xt_lo")
        wl_hi = sem("wl_hi")
        wl_lo = sem("wl_lo")
        logits = sem("logits")
        to_act = sem("to_act")
        to_dve = sem("to_dve")
        g_made = sem("g_made")
        cums = sem("cums")
        gcum_made = sem("gcum_made")
        gtr = sem("gtr")
        gt_copied = sem("gt_copied")
        gate_made = sem("gate_made")
        gate_tr = sem("gate_tr")
        gateT_made = sem("gateT_made")
        b3_in = sem("b3_in")
        b3_done = sem("b3_done")
        b3_added = sem("b3_added")
        f_up = sem("f_up")
        f_bias = sem("f_bias")
        f_act = sem("f_act")
        f_silu = sem("f_silu")
        f_mul = sem("f_mul")
        f_hi = sem("f_hi")
        f_lo = sem("f_lo")
        f_down = sem("f_down")
        f_acc = sem("f_acc")

        def value(name, s, half, k):
            n = per_step[name]
            if name in LAGGED:
                s = s + half
            return n * (s + 1) + k

        class At:

            def __init__(self, eng, s, half):
                self.eng, self.s, self.half = eng, s, half

            def wait(self, name, k):
                self.put(S[name], value(name, self.s, self.half, k))

            def before(self, name, k):
                self.put(S[name], value(name, self.s, self.half, k - per_step[name]))

            def put(self, semaphore, count):
                if self.eng is nc.sync:
                    hold(self.eng, semaphore, count)
                else:
                    self.eng.wait_ge(semaphore, count)

        def piece_base(half):
            return half * HALF_PIECES

        NPH = 3

        def hold(eng, semaphore, count):
            eng.wait_ge(semaphore, count)
            eng.sem_inc(passed, 1)

        def end_phase(eng, half, k):
            eng.drain().then_inc(phase, 1)
            hold(eng, phase, half * (4 * NPH) + 4 * (k + 2))

        def wkvflat(t, j):
            return t[:, 2 * j:2 * j + 2, :].rearrange("p a b -> p (a b)")

        HH, HL = [vwh, sth], [vwl, stl]
        FW = [(wqfh, wqfl), (wgfh, wgfl)]

        def z_lo(pool, at, c):
            at.wait("zhi", c + 1)
            nc.gpsimd.tensor_tensor(zl[:], yb[:, c, :], zh[:].bitcast(F32), ALU.subtract).then_inc(S["zlo"], 1)

        block = ctx.enter_context(nc.Block())

        @block.sync
        def _(sp):
            for name, n in per_step.items():
                sp.sem_inc(S[name], n)
            sp.sem_inc(wsplit_lo, 2)
            sp.sem_inc(f_mul, 2)
            sp.sem_inc(f_lo, 2)
            sp.sem_inc(f_down, 4)
            sp.sem_inc(phase, 4)
            sp.sem_inc(out_done, 32)
            sp.sem_inc(f_acc, 4)
            for dst, src in ((cosb[:], cos), (sinb[:], sin), (dtbb[:], dtb.partition_broadcast(P)),
                             (nA[:], alog.partition_broadcast(P)), (rbb[:], rb.partition_broadcast(P)),
                             (rbiasb[:], rbias.partition_broadcast(P)), (gn[:], gnw), (b1t[:], b1), (b2t[:], b2)):
                sp.dma_start(dst, src).then_inc(const_in, 16)

            def piece(half, n, src):
                hold(sp, wsplit_lo, piece_base(half) + n[0] + 1)
                sp.dma_start(stage[:, n[1], 0:src.shape[-1]], src).then_inc(stg[n[1]], 16)

            with sp.Fori(0, HALVES) as half:
                hold(sp, out_done, (half + 1) * 32)
                xv = x[bass.ds(half, 1), :, :, :].rearrange("o t p n -> p (o t) n")
                for j in range(2):
                    sp.dma_start(acc[:, 4 * j:4 * j + 4, :], xv[:, 4 * j:4 * j + 4, :]).then_inc(x_in[j], 16)
                hold(sp, phase, half * (4 * NPH) + 4)
                sp.wait_ge(const_made, CONSTS)
                sp.dma_start(wlraw, wlog).then_inc(wl_in, 16)
                sp.dma_start(b3t, b3).then_inc(b3_in, 16)
                for j in range(2):
                    piece(half, (j, j % 2), wkv[0, j])
                for j in range(4):
                    piece(half, (2 + j, j % 2), wq[0, j])
                for a in range(2):
                    hold(sp, gt_copied, half * 2 + a + 1)
                    for t in range(4):
                        sp.dma_start(gdram[bass.ds(half, 1), :, 4 * a + t, :].rearrange("o h i -> (o h) i"),
                                     gT[t * H:(t + 1) * H, a, :]).then_inc(g_out, 16)
                hold(sp, g_out, (half + 1) * (16 * 8))
                hold(sp, phase, half * (4 * NPH) + 8)

                with sp.Fori(0, KV) as kv:
                    kvn = (kv + 1) % KV
                    for b in range(ROWS):
                        s = half * STEPS + kv * ROWS + b
                        at = At(sp, s, half)

                        def gload(c):
                            if c < 2:
                                at.before("expg", c + 2)
                                at.before("gmask", c + 3)
                            elif c == 2:
                                at.wait("gmask", 1)
                            else:
                                at.wait("expg", 1)
                                at.wait("gmask", 2)
                            src = gdram[bass.ds(half, 1), bass.ds(kv * HG, HG), b * NCH + c, :]
                            src = src.rearrange("o h i -> (o h) i").partition_broadcast(P)
                            sp.dma_start(gbc[:, c % 2, :].rearrange("p (h i) -> p h i", h=HG), src).then_inc(
                                gb_in[c % 2], 16)

                        def att_piece(j, src):
                            piece(half, (6 + kv * 14 + j, j % 2), src)

                        def row(w, k, j):
                            return w[bass.ds(k, 1), j].rearrange("o p n -> (o p) n")

                        if b == 0:
                            gload(0)
                            att_piece(0, row(wg, kv, 0))
                            att_piece(1, row(wg, kv, 1))
                            gload(1)
                            att_piece(2, row(wg, kv, 2))
                            att_piece(3, row(wg, kv, 3))
                            gload(2)
                            att_piece(4, row(wo, kv, 0))
                            att_piece(5, row(wo, kv, 1))
                            gload(3)
                        else:
                            gload(0)
                            gload(1)
                            att_piece(6, row(wo, kv, 2))
                            att_piece(7, row(wo, kv, 3))
                            gload(2)
                            att_piece(8, row(wkv, kvn, 0))
                            att_piece(9, row(wkv, kvn, 1))
                            att_piece(10, row(wq, kvn, 0))
                            att_piece(11, row(wq, kvn, 1))
                            gload(3)
                            att_piece(12, row(wq, kvn, 2))
                            att_piece(13, row(wq, kvn, 3))
                def ffn_pieces(e, n0):
                    for i in range(4):
                        piece(half, (ATT_PIECES + n0 + i, i % 2),
                              w123[bass.ds(e, 1), :, i * PW:(i + 1) * PW].rearrange("o p n -> (o p) n"))

                ffn_pieces(0, 0)
                with sp.Fori(0, SLICES // 2) as ep:
                    for j in range(2):
                        ffn_pieces((ep * 2 + j + 1) % SLICES, ep * 8 + 4 * j + 4)
                hold(sp, phase, half * (4 * NPH) + 16)
                ov = out[bass.ds(half, 1), :, :, :].rearrange("o t p n -> p (o t) n")
                for j in range(2):
                    sp.dma_start(ov[:, 4 * j:4 * j + 4, :], acc[:, 4 * j:4 * j + 4, :]).then_inc(out_done, 16)
            sp.wait_ge(out_done, (HALVES + 1) * 32)

        @block.gpsimd
        def _(pool):
            g = nc.gpsimd
            made = [0]

            def link(ins):
                made[0] += 1
                ins.then_inc(const_made, 1)
                pool.wait_ge(const_made, made[0])

            for t, v in ((ones, 1.0), (ident, 0.0), (upper, 1.0), (amask, 0.0), (before, 1.0), (lneps, LN_EPS),
                         (rmseps, RMS_EPS), (one, 1.0), (gate18, 1.0), (rs, 1.0)):
                link(g.memset(t[:], v))
            for t in (woh, wol):
                link(g.memset(t[:].bitcast(F32), 0.0))
            link(g.affine_select(out=ident[:], in_=ident[:], compare_op=ALU.not_equal, fill=1.0, base=0,
                                 pattern=[[-1, P]], channel_multiplier=1))
            link(g.affine_select(out=upper[:], in_=upper[:], compare_op=ALU.is_ge, fill=0.0, base=0,
                                 pattern=[[1, P]], channel_multiplier=-1))
            link(g.affine_select(out=amask[:], in_=amask[:], compare_op=ALU.is_ge, fill=MASKED, base=0,
                                 pattern=[[1, P]], channel_multiplier=-1))
            link(g.affine_select(out=before[:], in_=before[:], compare_op=ALU.is_gt, fill=0.0, base=0,
                                 pattern=[[1, E], [-1, E]], channel_multiplier=0))

            def split_lo(half, n, hi_out, lo_out):
                pool.wait_ge(wsplit_hi, piece_base(half) + n[0] + 1)
                g.tensor_tensor(lo_out, stage[:, n[1], 0:lo_out.shape[-1]], hi_out.bitcast(F32), ALU.subtract).then_inc(wsplit_lo, 1)

            with pool.Fori(0, HALVES) as half:
                for j in range(2):
                    split_lo(half, (j, j % 2), wkvflat(wkvh, j), wkvflat(wkvl, j))
                for j in range(4):
                    split_lo(half, (2 + j, j % 2), wqh[:, j, :], wql[:, j, :])
                end_phase(pool, half, 0)
                with pool.Fori(0, KV) as kv:
                    for b in range(ROWS):
                        s = half * STEPS + kv * ROWS + b
                        at = At(pool, s, half)

                        def w_lo(j, hi_out, lo_out):
                            split_lo(half, (6 + kv * 14 + j, j % 2), hi_out, lo_out)

                        def gmasked(c):
                            pool.wait_ge(gb_in[c % 2], (s * 2 + c // 2 + 1) * 16)
                            if c < 2:
                                at.before("wlo", c + 3)
                            else:
                                at.wait("wlo", c - 1)
                            g.tensor_tensor(gm[:, c % 2, :].rearrange("p (h i) -> p h i", h=HG),
                                            gbc[:, c % 2, :].rearrange("p (h i) -> p h i", h=HG),
                                            amask[:].unsqueeze(1).broadcast_to([P, HG, P]),
                                            ALU.add).then_inc(S["gmask"], 1)

                        def rope_lo(i, hi, lo):
                            at.wait("ropehi", i + 1)
                            g.tensor_tensor(lo, t2[:, (5 * b + i) % 2, :], hi.bitcast(F32),
                                            ALU.subtract).then_inc(S["ropelo"], 1)

                        gmasked(0)
                        gmasked(1)
                        rope_lo(0, kh[:], kl[:])
                        for j in range(4):
                            if j == 1:
                                at.wait("vhi", 1)
                                g.tensor_tensor(vl[:], vf[:], vh[:].bitcast(F32), ALU.subtract).then_inc(S["vlo"], 1)
                            rope_lo(j + 1, qh[:, j, :], ql[:, j, :])
                            if b == 0:
                                w_lo(j, wgh[:, j, :], wgl[:, j, :])
                            else:
                                w_lo(4 + j, woh[:, j, :], wol[:, j, :])
                        for c in range(NCH):
                            z_lo(pool, at, c)
                            if c < 2:
                                gmasked(c + 2)
                            if b == 1 and c < 3:
                                for j in (2 * c, 2 * c + 1):
                                    if j < 2:
                                        w_lo(8 + j, wkvflat(wkvh, j), wkvflat(wkvl, j))
                                    else:
                                        w_lo(8 + j, wqh[:, j - 2, :], wql[:, j - 2, :])
                at = At(pool, half * STEPS + STEPS, half)
                for c in range(NCH):
                    z_lo(pool, at, c)
                end_phase(pool, half, 1)
                def ffn_lo(j, n0):
                    for i in range(4):
                        o = slice(i * PW, (i + 1) * PW)
                        split_lo(half, (ATT_PIECES + n0 + i, i % 2), FW[j][0][:, o], FW[j][1][:, o])

                ffn_lo(0, 0)
                with pool.Fori(0, SLICES // 2) as ep:
                    for j in range(2):
                        for blk in range(2):
                            f = half * BLOCKS + ep * 4 + 2 * j + blk
                            pool.wait_ge(f_hi, f + 1)
                            g.tensor_tensor(HL[blk][:], gm[:, blk, :], HH[blk][:].bitcast(F32),
                                            ALU.subtract).then_inc(f_lo, 1)
                            if blk == 0:
                                ffn_lo(1 - j, ep * 8 + 4 * j + 4)
                end_phase(pool, half, 2)

        @block.scalar
        def _(act):
            a = nc.scalar

            def split_hi(half, n, hi_out, scale=None):
                act.wait_ge(stg[n[1]], ((piece_base(half) + n[0] - n[1]) // 2 + 1) * 16)
                if scale is not None:
                    src = stage[:, n[1], 0:hi_out.shape[-1]]
                    a.activation(src, src, ACT.Copy, scale=scale[0]).then_inc(wscaled, 1)
                    act.wait_ge(wscaled, scale[1])
                a.activation(hi_out, stage[:, n[1], 0:hi_out.shape[-1]], ACT.Copy).then_inc(wsplit_hi, 1)

            act.wait_ge(const_in, 16 * CONST_DMAS)
            act.wait_ge(const_made, CONSTS)
            a.activation(gn[:], gn[:], ACT.Copy, scale=0.5).then_inc(aseq, 1)
            a.activation(b1t[:], b1t[:], ACT.Copy, scale=0.5).then_inc(aseq, 1)
            a.activation(nA[:], nA[:], ACT.Exp).then_inc(aseq, 1)
            act.wait_ge(aseq, 3)
            with act.Fori(0, HALVES) as half:
                act.wait_ge(wl_in, (half + 1) * 16)
                a.activation(wlh, wlraw, ACT.Copy).then_inc(wl_hi, 1)
                act.wait_ge(ln_stats, half + 1)
                a.activation(rstd[:], mv[:, :, 1], ACT.Sqrt, bias=lneps[:, 0:1]).then_inc(ln_std, 1)
                for t in range(NT):
                    act.wait_ge(xt_tr, half * NT + t + 1)
                    a.activation(xnh[:, :, t * P:(t + 1) * P], PJ[t % 2][:].rearrange("p (k n) -> p k n", k=KC),
                                 ACT.Copy).then_inc(xt_hi, 1)
                for j in range(2):
                    split_hi(half, (j, j % 2), wkvflat(wkvh, j))
                for j in range(4):
                    split_hi(half, (2 + j, j % 2), wqh[:, j, :])
                act.wait_ge(to_act, half * 4 + 1)
                a.activation(sm, sm, ACT.Exp).then_inc(to_dve, 1)
                act.wait_ge(to_act, half * 4 + 2)
                a.activation(ee, ee, ACT.Exp, scale=-1.0).then_inc(to_dve, 1)
                act.wait_ge(to_act, half * 4 + 3)
                a.activation(ll, uu, ACT.Ln).then_inc(to_dve, 1)
                act.wait_ge(to_act, half * 4 + 4)
                a.activation(wdec, wdec, ACT.Exp).then_inc(to_dve, 1)
                a.activation(cdec, cdec, ACT.Exp).then_inc(to_dve, 1)
                end_phase(act, half, 0)

                def rms_batch(at, half):
                    at.before("ssqc", 4)
                    a.activation(rs[:], rs[:], ACT.Ln, scale=1.0 / D, bias=rmseps[:, 0:1]).then_inc(S["rsln"], 1)
                    at.wait("rsln", 1)
                    a.activation(rs[:], rs[:], ACT.Exp, scale=-0.5).then_inc(S["rms"], 1)

                def z_hi(at, c):
                    at.wait("z", c + 1)
                    if c == 0:
                        at.before("oproj", 4)
                    else:
                        at.wait("oproj", c)
                    a.activation(zh[:], yb[:, c, :], ACT.Copy).then_inc(S["zhi"], 1)

                with act.Fori(0, KV) as kv:
                    for b in range(ROWS):
                        s = half * STEPS + kv * ROWS + b
                        at = At(act, s, half)

                        def w_hi(j, hi_out, scale=None):
                            split_hi(half, (6 + kv * 14 + j, j % 2), hi_out, scale)

                        def head(kind, c, h):
                            return hcoef[:, b, kind, c, h:h + 1]

                        def rope_hi(i, hi):
                            at.wait("rope", i + 1)
                            a.activation(hi, t2[:, (5 * b + i) % 2, :], ACT.Copy).then_inc(S["ropehi"], 1)

                        def decay(c):
                            at.wait("gmask", c + 1)
                            for h in range(HG):
                                gv = gm[:, c % 2, h * P:(h + 1) * P]
                                ins = a.activation(gv, gv, ACT.Exp, bias=head(0, c, h))
                            ins.then_inc(S["dec"], 1)

                        def exp_g(c):
                            at.wait("zlo", c + 1)
                            a.activation(yb[:, c, :], gbc[:, c % 2, :], ACT.Exp).then_inc(S["expg"], 1)

                        def vw_hi(c):
                            if c:
                                at.wait("cstate", c)
                            for h in range(HG):
                                ins = a.activation(vwh[:, h * P:(h + 1) * P], vf[:, c * P:(c + 1) * P], ACT.Copy,
                                                   scale=head(2, c, h))
                            ins.then_inc(S["vwhi"], 1)

                        at.wait("proj", 2)
                        a.activation(y2[:], PJ[1][:], ACT.Copy).then_inc(S["vraw"], 1)
                        rope_hi(0, kh[:])
                        rope_hi(1, qh[:, 0, :])
                        at.wait("tr", 1)
                        a.activation(vf[:], TR[:], ACT.Copy)
                        a.activation(vh[:], TR[:], ACT.Copy).then_inc(S["vhi"], 1)
                        rms_batch(at, half)
                        at.wait("tr", 2)
                        a.activation(knh[:], TR[:, 0:3 * P].rearrange("p (a b) -> p a b", a=3),
                                     ACT.Copy).then_inc(S["knhi"], 1)
                        for j in range(1, 4):
                            rope_hi(j + 1, qh[:, j, :])
                            for i in ((0, 1) if j == 1 else (j,)):
                                if b == 0:
                                    w_hi(i, wgh[:, i, :])
                                else:
                                    w_hi(4 + i, woh[:, i, :], (gn[:, 0:1], (half * KV + kv) * HG + i + 1))
                        at.wait("coef", 1)
                        decay(0)
                        vw_hi(0)
                        z_hi(at, 0)
                        for c in range(NCH):
                            if c:
                                z_hi(at, c)
                            at.wait("wsc", c + 1)
                            if c:
                                at.wait("yintra", c)
                            a.activation(wfh[:], gm[:, c % 2, :], ACT.Copy).then_inc(S["whi"], 1)
                            at.wait("proj", 7 + c)
                            at.before("u", 4)
                            a.activation(gate[:, c, :], PJ[c % 2][:], ACT.Tanh, scale=0.5).then_inc(S["tanh"], 1)
                            if c:
                                exp_g(c)
                            if c < 3:
                                at.wait("stt", c + 1)
                                if c:
                                    at.wait("yinter", c)
                                a.activation(sth[:], st[:], ACT.Copy).then_inc(S["sthi"], 1)
                                decay(c + 1)
                                if c < 2:
                                    vw_hi(c + 1)
                                if b == 1:
                                    for j in (2 * c, 2 * c + 1):
                                        w_hi(8 + j, wkvflat(wkvh, j) if j < 2 else wqh[:, j - 2, :])
                            if c:
                                at.wait("ssq", c)
                                a.activation(rs[:, c - 1, :], TR[:], ACT.Copy).then_inc(S["ssqc"], 1)
                            at.wait("y", c + 1)
                            a.activation(y2[:], yb[:, c, :], ACT.Square).then_inc(S["ysq"], 1)
                        at.wait("ssq", 4)
                        a.activation(rs[:, 3, :], TR[:], ACT.Copy).then_inc(S["ssqc"], 1)
                at = At(act, half * STEPS + STEPS, half)
                rms_batch(at, half)
                for c in range(NCH):
                    z_hi(at, c)
                end_phase(act, half, 1)

                def ffn_hi(j, n0):
                    for i in range(4):
                        split_hi(half, (ATT_PIECES + n0 + i, i % 2), FW[j][0][:, i * PW:(i + 1) * PW])

                ffn_hi(0, 0)
                with act.Fori(0, SLICES // 2) as ep:
                    for j in range(2):
                        for blk in range(2):
                            f = half * BLOCKS + ep * 4 + 2 * j + blk
                            bias = fb1[:, j:j + 1]
                            up = [PJ[0], TR][blk]
                            act.wait_ge(f_up, f + 1)
                            act.wait_ge(f_bias, half * (SLICES // 2) + ep + 1)
                            act.wait_ge(f_lo, f + 1)
                            a.activation(t2[:, blk, :], up[:], ACT.Identity, scale=0.5, bias=bias)
                            a.activation(gm[:, blk, :], up[:], ACT.Tanh, scale=0.5, bias=bias).then_inc(f_act, 1)
                            act.wait_ge(f_mul, f + 3)
                            act.wait_ge(f_down, (f + half) * 4 + 4)
                            a.activation(HH[blk][:], gm[:, blk, :], ACT.Copy).then_inc(f_hi, 1)
                            if blk == 0:
                                act.wait_ge(f_down, (f + half) * 4 + 8)
                                ffn_hi(1 - j, ep * 8 + 4 * j + 4)
                end_phase(act, half, 2)

        @block.tensor
        def _(pe):
            def mm3(out_, a_hi, a_lo, b_hi, b_lo, first, last):
                nc.tensor.matmul(out_, a_hi, b_hi, start=first, stop=False)
                nc.tensor.matmul(out_, a_hi, b_lo, start=False, stop=False)
                return nc.tensor.matmul(out_, a_lo, b_hi, start=False, stop=last)

            pe.wait_ge(const_made, CONSTS)
            pe.wait_ge(const_in, 16 * CONST_DMAS)
            with pe.Fori(0, HALVES) as half:
                for t in range(NT):
                    pe.wait_ge(xt_made, half * NT + t + 1)
                    if t >= 2:
                        pe.wait_ge(xt_lo, half * NT + t - 1)
                    for k in range(KC):
                        ins = nc.tensor.transpose(PJ[t % 2][:, k * P:(k + 1) * P], t2[:, t % 2, k * P:(k + 1) * P],
                                                  ident[:])
                    ins.then_inc(xt_tr, 1)
                pe.wait_ge(wl_lo, half + 1)
                for t in range(NT):
                    pe.wait_ge(xt_lo, half * NT + t + 1)
                    ts = slice(t * P, (t + 1) * P)
                    for k in range(KC):
                        ins = mm3(CS[:, t * LW:(t + 1) * LW], xnh[:, k, ts], xnl[:, k, ts], wlh[:, k, :], wll[:, k, :],
                                  k == 0, k == KC - 1)
                ins.then_inc(logits, 1)
                pe.wait_ge(g_made, half + 1)
                nc.tensor.matmul(SC[:, 0:NH8], upper[:], gg.rearrange("p t n -> p (t n)"), start=True, stop=True)
                nc.tensor.matmul(YI[:, 0:NH8], ones[:], gg.rearrange("p t n -> p (t n)"), start=True,
                                 stop=True).then_inc(cums, 1)
                pe.wait_ge(gcum_made, half + 1)
                for i in range(2):
                    ins = nc.tensor.transpose(YE[:, i * P:(i + 1) * P], gcum[:, i * P:(i + 1) * P], ident[:])
                ins.then_inc(gtr, 1)
                pe.wait_ge(gate_made, half + 1)
                pe.wait_ge(b3_in, (half + 1) * 16)
                for t in range(NT):
                    if t:
                        pe.wait_ge(gateT_made, half * NT + t)
                    nc.tensor.transpose(OU[0:E + 1, 0:P], gate18[:, t, 1:E + 2], ident[:]).then_inc(gate_tr, 1)
                    pe.wait_ge(gateT_made, half * NT + t + 1)
                    if t:
                        pe.wait_ge(b3_added, half * NT + t)
                    nc.tensor.matmul(PJ[0][:], gateT, b3t, start=True, stop=True).then_inc(b3_done, 1)
                end_phase(pe, half, 0)

                def out_proj(at, c, row):
                    at.wait("zlo", c + 1)
                    if c == 0:
                        at.before("accd", 4)
                    else:
                        at.wait("accd", c)
                    for h in range(HG):
                        hs = slice(h * P, (h + 1) * P)
                        ins = mm3(OU[:], zh[:, hs], zl[:, hs], woh[:, h, :], wol[:, h, :], h == 0, h == HG - 1)
                    ins.then_inc(S["oproj"], 1)

                with pe.Fori(0, KV) as kv:
                    for b in range(ROWS):
                        s = half * STEPS + kv * ROWS + b
                        at = At(pe, s, half)
                        rows = slice(b * L, (b + 1) * L)

                        def weights(n):
                            pe.wait_ge(wsplit_lo, piece_base(half) + kv * 14 + 6 + n + 2)

                        def project(bank, wh_, wl_):
                            for k in range(KC):
                                ins = mm3(PJ[bank][:], wh_[k], wl_[k], xnh[:, k, rows], xnl[:, k, rows], k == 0,
                                          k == KC - 1)
                            ins.then_inc(S["proj"], 1)

                        def proj_q(j):
                            hs = slice(j * P, (j + 1) * P)
                            project(j % 2, [wqh[:, k, hs] for k in range(KC)], [wql[:, k, hs] for k in range(KC)])

                        def proj_g(j):
                            hs = slice(j * P, (j + 1) * P)
                            project(j % 2, [wgh[:, k, hs] for k in range(KC)], [wgl[:, k, hs] for k in range(KC)])

                        def scores(c):
                            if c == 0:
                                at.before("wsc", 4)
                            else:
                                at.wait("wsc", c)
                            cs = slice(c * P, (c + 1) * P)
                            mm3(SC[:].rearrange("p (h i) -> p h i", h=HG), kh[:, cs], kl[:, cs], qh[:, :, cs],
                                ql[:, :, cs], True, True).then_inc(S["score"], 1)

                        def chunk_state(c):
                            at.wait("vwlo", c + 1)
                            if c == 0:
                                at.before("stt", 3)
                            else:
                                at.wait("stt", c)
                            mm3(CS[:], knh[:, c, :], knl[:, c, :], vwh[:], vwl[:], True, True).then_inc(S["cstate"], 1)

                        def inter(c):
                            at.wait("stlo", c)
                            if c == 1:
                                at.before("yt", 3)
                            else:
                                at.wait("yt", c - 1)
                            cs = slice(c * P, (c + 1) * P)
                            for h in range(HG):
                                hs = slice(h * P, (h + 1) * P)
                                ins = mm3(YE[:, hs], sth[:, hs], stl[:, hs], qh[:, h, cs], ql[:, h, cs], True, True)
                            ins.then_inc(S["yinter"], 1)

                        def intra(c):
                            at.wait("wlo", c + 1)
                            if c == 0:
                                at.wait("vlo", 1)
                                at.before("y", 4)
                            else:
                                at.wait("y", c)
                            cs = slice(c * P, (c + 1) * P)
                            mm3(YI[:], vh[:, cs], vl[:, cs], wfh[:], wfl[:], True, True).then_inc(S["yintra"], 1)

                        def squares(c):
                            at.wait("ysq", c + 1)
                            if c:
                                at.wait("ssqc", c)
                            nc.tensor.matmul(TR[:], ones[:], y2[:], start=True, stop=True).then_inc(S["ssq"], 1)

                        if b == 0:
                            weights(-4)
                        at.before("gated", 3)
                        project(0, [wkvh[:, k, 0:P] for k in range(KC)], [wkvl[:, k, 0:P] for k in range(KC)])
                        at.before("gated", 4)
                        project(1, [wkvh[:, k, P:2 * P] for k in range(KC)], [wkvl[:, k, P:2 * P] for k in range(KC)])
                        if b == 0:
                            weights(0)
                        at.wait("roperd", 1)
                        proj_q(0)
                        at.wait("vraw", 1)
                        at.before("ssqc", 4)
                        for i in range(4):
                            ins = nc.tensor.transpose(TR[:, i * P:(i + 1) * P], y2[:, i * P:(i + 1) * P], ident[:])
                        ins.then_inc(S["tr"], 1)
                        proj_q(1)
                        at.wait("rope", 1)
                        at.wait("vhi", 1)
                        for i in range(3):
                            ins = nc.tensor.transpose(TR[:, i * P:(i + 1) * P], t2[:, (5 * b) % 2, i * P:(i + 1) * P],
                                                      ident[:])
                        ins.then_inc(S["tr"], 1)
                        for j in (2, 3):
                            at.wait("roperd", j)
                            proj_q(j)
                        at.wait("knlo", 1)
                        at.wait("knhi", 1)
                        at.wait("ropelo", 5)
                        scores(0)
                        for c in range(NCH):
                            if b == 0:
                                weights(4)
                            if c < 2:
                                at.wait("roperd", 4 + c)
                            else:
                                at.wait("gated", c - 1)
                            proj_g(c)
                            if c < 3:
                                chunk_state(c)
                            if c:
                                inter(c)
                            if c < 3:
                                scores(c + 1)
                            intra(c)
                            if c:
                                squares(c - 1)
                            if b == 1:
                                weights(8)
                            out_proj(at, c, 1 - b)
                        squares(3)
                at = At(pe, half * STEPS + STEPS, half)
                for c in range(NCH):
                    out_proj(at, c, 1)
                end_phase(pe, half, 1)

                def down(f, blk, j):
                    pe.wait_ge(f_lo, f + 2)
                    for t, bank in enumerate((SC, YI, YE, OU)):
                        ts = slice(t * P, (t + 1) * P)
                        pe.wait_ge(f_acc, (f + half) * 4 + t + 1)
                        mm3(bank[:], HH[blk][:, ts], HL[blk][:, ts], FW[j][0][:, 1024:1536], FW[j][1][:, 1024:1536],
                            True, True).then_inc(f_down, 1)

                with pe.Fori(0, SLICES // 2) as ep:
                    for j in range(2):
                        pe.wait_ge(wsplit_lo, piece_base(half) + ATT_PIECES + ep * 8 + 4 * j + 4 + 2)
                        for blk in range(2):
                            f = half * BLOCKS + ep * 4 + 2 * j + blk
                            pe.wait_ge(f_mul, f + 1)
                            rows = slice(blk * L, (blk + 1) * L)
                            for i, bank in enumerate(([PJ[0], PJ[1]], [TR, CS])[blk]):
                                for k in range(KC):
                                    ws = slice(i * 512 + k * P, i * 512 + (k + 1) * P)
                                    ins = mm3(bank[:], FW[j][0][:, ws], FW[j][1][:, ws], xnh[:, k, rows],
                                              xnl[:, k, rows], k == 0, k == KC - 1)
                            ins.then_inc(f_up, 1)
                            down(f, 1 - blk, j if blk else 1 - j)
                down((half + 1) * BLOCKS, 1, 1)
                end_phase(pe, half, 2)

        @block.vector
        def _(dve):
            v = nc.vector
            PRO = 64
            dve.wait_ge(const_made, CONSTS)
            dve.wait_ge(const_in, 16 * CONST_DMAS)
            with dve.Fori(0, HALVES) as half:
                n = [0]

                def link(ins):
                    n[0] += 1
                    ins.then_inc(dseq, 1)
                    dve.wait_ge(dseq, half * PRO + n[0])

                for t in range(NT):
                    if t % 4 == 0:
                        dve.wait_ge(x_in[t // 4], (half + 1) * 16)
                    ins = v.bn_stats(bst[:, t, :], acc[:, t, :])
                link(ins)
                v.memset(gate18[:, :, 0], 0.0)
                for t in range(NT):
                    ins = v.bn_aggr(mv[:, t, :], bst[:, t, :])
                ins.then_inc(ln_stats, 1)
                dve.wait_ge(ln_std, half + 1)
                link(v.reciprocal(rstd[:], rstd[:]))

                def normalise(t):
                    if t >= 2:
                        dve.wait_ge(xt_tr, half * NT + t - 1)
                    v.tensor_scalar(t2[:, t % 2, :], acc[:, t, :], mv[:, t, 0:1], rstd[:, t:t + 1], ALU.subtract,
                                    ALU.mult).then_inc(xt_made, 1)

                normalise(0)
                for t in range(NT):
                    if t + 1 < NT:
                        normalise(t + 1)
                    dve.wait_ge(xt_hi, half * NT + t + 1)
                    ts = slice(t * P, (t + 1) * P)
                    v.tensor_tensor(xnl[:, :, ts], PJ[t % 2][:].rearrange("p (k n) -> p k n", k=KC),
                                    xnh[:, :, ts].bitcast(F32), ALU.subtract).then_inc(xt_lo, 1)
                    if t == 0:
                        dve.wait_ge(wl_hi, half + 1)
                        v.tensor_tensor(wll, wlraw, wlh.bitcast(F32), ALU.subtract).then_inc(wl_lo, 1)

                def bc(ap, shape, axis):
                    return ap.unsqueeze(axis).broadcast_to(shape)

                dve.wait_ge(logits, half + 1)
                link(v.tensor_copy(gflat[:, 0:NT * LW], CS[:, 0:NT * LW]))
                lgr = lg[:, :, H:LW]
                link(v.tensor_tensor(lgr, lgr, bc(rbb[:], [P, NT, E], 1), ALU.add))
                link(v.tensor_reduce(mx1[:, :, 0], lgr, AX.X, ALU.max))
                v.tensor_tensor(sm, lgr, mx1.broadcast_to([P, NT, E]), ALU.subtract).then_inc(to_act, 1)
                link(v.tensor_tensor(zz, lg[:, :, 0:H], bc(dtbb[:], [P, NT, H], 1), ALU.add))
                link(v.tensor_scalar(dd, zz, -1.0, None, ALU.mult))
                v.tensor_tensor(ee, zz, dd, ALU.max).then_inc(to_act, 1)
                dve.wait_ge(to_dve, half * 5 + 2)
                link(v.tensor_scalar(uu, ee, 1.0, None, ALU.add))
                v.tensor_scalar(dd, uu, 1.0, None, ALU.subtract).then_inc(to_act, 1)
                dve.wait_ge(to_dve, half * 5 + 3)
                link(v.tensor_scalar(gg, dd, 0.0, None, ALU.is_equal))
                link(v.tensor_tensor(ll, ll, gg, ALU.add))
                link(v.tensor_tensor(dd, dd, gg, ALU.add))
                link(v.tensor_tensor(ll, ll, ee, ALU.mult))
                link(v.reciprocal(dd, dd))
                link(v.tensor_tensor(ll, ll, dd, ALU.mult))
                link(v.scalar_tensor_tensor(dt, zz, 0.0, ll, ALU.max, ALU.add))
                link(v.tensor_tensor(gg, dt, bc(nA[:], [P, NT, H], 1), ALU.mult))
                v.tensor_scalar(gg, gg, -1.0, None, ALU.mult).then_inc(g_made, 1)
                dve.wait_ge(cums, half + 1)
                link(v.tensor_copy(gcum, SC[:, 0:NH8]))
                gc3 = gcum.rearrange("p (t n) -> p t n", t=NT)
                last3 = YI[:, 0:NH8].rearrange("p (t n) -> p t n", t=NT)
                v.tensor_scalar(negG, gc3, -1.0, None, ALU.mult).then_inc(gcum_made, 1)
                v.tensor_tensor(wdec, last3, gc3, ALU.subtract)
                v.tensor_copy(cdec, last3).then_inc(to_act, 1)
                for i in range(2):
                    if i == 0:
                        dve.wait_ge(gtr, half + 1)
                    v.tensor_copy(gT[:, i, :], YE[:, i * P:(i + 1) * P]).then_inc(gt_copied, 1)

                link(v.tensor_reduce(sum1[:, :, 0], sm, AX.X, ALU.add))
                link(v.reciprocal(rcp1, sum1))
                link(v.tensor_tensor(sc_, sm, rcp1.broadcast_to([P, NT, E]), ALU.mult))
                link(v.tensor_tensor(sc_, sc_, bc(rbiasb[:], [P, NT, E], 1), ALU.add))

                def ranks(out_, vals, m, t0, nt):
                    w = nt * m * m
                    gt = yflat[:, 0:w].rearrange("p (t a b) -> p t a b", t=nt, a=m)
                    eq = yflat[:, 1024:1024 + w].rearrange("p (t a b) -> p t a b", t=nt, a=m)
                    vt = vals[:, t0:t0 + nt, :]
                    shape = [P, nt, m, m]
                    link(v.tensor_tensor(gt, bc(vt, shape, 2), bc(vt, shape, 3), ALU.is_gt))
                    link(v.tensor_tensor(eq, bc(vt, shape, 2), bc(vt, shape, 3), ALU.is_equal))
                    link(v.tensor_tensor(eq, eq, bc(before[:, 0:m, 0:m], shape, 1), ALU.mult))
                    link(v.tensor_tensor(gt, gt, eq, ALU.add))
                    link(v.tensor_reduce(out_[:, t0:t0 + nt, :], gt, AX.X, ALU.add))

                link(v.tensor_reduce(gmx, sc_.rearrange("p t (g e) -> p t g e", g=GROUPS), AX.X, ALU.max))
                ranks(grk, gmx, GROUPS, 0, NT)
                link(v.tensor_scalar(keep, grk, 2.0, None, ALU.is_lt))
                link(v.tensor_scalar(keep, keep, -MASKED, MASKED, ALU.mult, ALU.add))
                link(v.tensor_tensor(mk.rearrange("p t (g e) -> p t g e", g=GROUPS),
                                     sc_.rearrange("p t (g e) -> p t g e", g=GROUPS),
                                     bc(keep, [P, NT, GROUPS, EG], 3), ALU.add))
                ranks(rk, mk, E, 0, 4)
                ranks(rk, mk, E, 4, 4)
                v.scalar_tensor_tensor(gate18[:, :, 1:E + 1], rk, 2.0, sc_, ALU.is_lt, ALU.mult).then_inc(gate_made, 1)
                dve.wait_ge(to_dve, half * 5 + 5)
                v.tensor_tensor(wdec, wdec, dt, ALU.mult)
                for t in range(NT):
                    dve.wait_ge(gate_tr, half * NT + t + 1)
                    if t:
                        dve.wait_ge(b3_done, half * NT + t)
                    v.tensor_copy(gateT, OU[0:E + 1, 0:P]).then_inc(gateT_made, 1)
                    dve.wait_ge(b3_done, half * NT + t + 1)
                    v.tensor_tensor(acc[:, t, :], acc[:, t, :], PJ[0][:], ALU.add).then_inc(b3_added, 1)
                v.memset(yb[:], 0.0)
                v.memset(rs[:], 1.0)
                assert n[0] <= PRO
                dve.sem_inc(dseq, PRO - n[0])
                end_phase(dve, half, 0)

                def late_z(at, c):
                    at.wait("rms", 1)
                    at.before("u", c + 1)
                    v.tensor_tensor(yb[:, c, :], yb[:, c, :], rs[:, c, :], ALU.mult).then_inc(S["z"], 1)

                def late_acc(at, c, row):
                    at.wait("oproj", c + 1)
                    tile = acc[:, row * NCH + c, :]
                    v.tensor_tensor(tile, tile, OU[:], ALU.add).then_inc(S["accd"], 1)

                with dve.Fori(0, KV) as kv:
                    for b in range(ROWS):
                        s = half * STEPS + kv * ROWS + b
                        at = At(dve, s, half)

                        def head(kind, c, h):
                            return hcoef[:, b, kind, c, h:h + 1]

                        def rope(i, bank):
                            slot = (5 * b + i) % 2
                            at.wait("proj", (1, 3, 4, 5, 6)[i])
                            if i < 2:
                                at.before("ropelo", 4 + i)
                            else:
                                at.wait("ropelo", i - 1)
                            if i == 2:
                                at.wait("tr", 2)
                            if i:
                                at.wait("rope", i)
                            else:
                                at.before("rope", 5)
                            hd = D // 2
                            v.tensor_tensor(t1[:], PJ[bank][:], cosb[:], ALU.mult)
                            v.tensor_tensor(t2[0:hd, slot, :], PJ[bank][hd:D, :], sinb[0:hd, :], ALU.mult)
                            v.tensor_tensor(t2[hd:D, slot, :], PJ[bank][0:hd, :], sinb[hd:D, :],
                                            ALU.mult).then_inc(S["roperd"], 1)
                            at.wait("roperd", i + 1)
                            v.tensor_tensor(t2[:, slot, :], t1[:], t2[:, slot, :], ALU.add).then_inc(S["rope"], 1)

                        def weigh(c):
                            at.wait("score", c + 1)
                            at.wait("dec", c + 1)
                            for h in range(HG):
                                hs = slice(h * P, (h + 1) * P)
                                ins = v.scalar_tensor_tensor(gm[:, c % 2, hs], SC[:, hs], head(1, c, h),
                                                             gm[:, c % 2, hs], ALU.mult, ALU.mult)
                            ins.then_inc(S["wsc"], 1)

                        def vw_lo(c):
                            at.wait("vwhi", c + 1)
                            for h in range(HG):
                                hs = slice(h * P, (h + 1) * P)
                                ins = v.scalar_tensor_tensor(vwl[:, hs], vf[:, c * P:(c + 1) * P], head(2, c, h),
                                                             vwh[:, hs].bitcast(F32), ALU.mult, ALU.subtract)
                            ins.then_inc(S["vwlo"], 1)

                        v.tensor_copy(hcoef[:, b], coef[:, :, b * NCH:(b + 1) * NCH, bass.ds(kv * HG, HG)]).then_inc(
                            S["coef"], 1)
                        at.wait("coef", 1)
                        rope(0, 0)
                        rope(1, 0)
                        rope(2, 1)
                        at.wait("knhi", 1)
                        v.tensor_tensor(knl[:], TR[:, 0:3 * P].rearrange("p (a b) -> p a b", a=3),
                                        knh[:].bitcast(F32), ALU.subtract).then_inc(S["knlo"], 1)
                        rope(3, 0)
                        rope(4, 1)
                        late_z(at, 0)
                        vw_lo(0)
                        weigh(0)
                        for c in range(NCH):
                            at.wait("whi", c + 1)
                            v.tensor_tensor(wfl[:], gm[:, c % 2, :], wfh[:].bitcast(F32),
                                            ALU.subtract).then_inc(S["wlo"], 1)
                            at.wait("tanh", c + 1)
                            v.scalar_tensor_tensor(gate[:, c, :], gate[:, c, :], 1.0, PJ[c % 2][:], ALU.add,
                                                   ALU.mult).then_inc(S["gated"], 1)
                            if c < 3:
                                at.wait("cstate", c + 1)
                                if c == 0:
                                    v.tensor_copy(st[:], CS[:]).then_inc(S["stt"], 1)
                                else:
                                    at.wait("sthi", c)
                                    at.wait("stt", c)
                                    for h in range(HG):
                                        hs = slice(h * P, (h + 1) * P)
                                        ins = v.scalar_tensor_tensor(st[:, hs], st[:, hs], head(3, c, h),
                                                                     CS[:, hs], ALU.mult, ALU.add)
                                    ins.then_inc(S["stt"], 1)
                            if c:
                                at.wait("yinter", c)
                                at.wait("expg", c)
                                v.tensor_tensor(yb[:, c, :], YE[:], yb[:, c, :], ALU.mult).then_inc(S["yt"], 1)
                            if c < 3:
                                at.wait("sthi", c + 1)
                                v.tensor_tensor(stl[:], st[:], sth[:].bitcast(F32), ALU.subtract).then_inc(
                                    S["stlo"], 1)
                                weigh(c + 1)
                                if c < 2:
                                    vw_lo(c + 1)
                            at.wait("yintra", c + 1)
                            if c:
                                at.wait("yt", c)
                                v.tensor_tensor(yb[:, c, :], YI[:], yb[:, c, :], ALU.add).then_inc(S["y"], 1)
                            else:
                                at.wait("zlo", 1)
                                v.tensor_copy(yb[:, 0, :], YI[:]).then_inc(S["y"], 1)
                            if c < 3:
                                late_z(at, c + 1)
                            late_acc(at, c, 1 - b)
                        for c in range(NCH):
                            at.wait("ysq", c + 1)
                            if c == 0:
                                at.wait("gated", 4)
                            yv = yb[:, c, :].rearrange("p (h i) -> p h i", h=HG)
                            v.tensor_tensor(yv, yv, gate[:, :, c * P:(c + 1) * P], ALU.mult).then_inc(S["u"], 1)
                at = At(dve, half * STEPS + STEPS, half)
                for c in range(NCH):
                    late_z(at, c)
                for c in range(NCH):
                    late_acc(at, c, 1)
                end_phase(dve, half, 1)

                def add_down(f, blk, col):
                    for t, bank in enumerate((SC, YI, YE, OU)):
                        dve.wait_ge(f_down, (f + half) * 4 + t + 5)
                        tile = acc[:, blk * NCH + t, :]
                        v.scalar_tensor_tensor(tile, bank[:], gate18[:, blk * NCH + t, bass.ds(col, 1)], tile,
                                               ALU.mult, ALU.add).then_inc(f_acc, 1)

                with dve.Fori(0, SLICES // 2) as ep:
                    v.tensor_copy(fb1[:], b1t[:, bass.ds(ep * 2, 2)]).then_inc(f_bias, 1)
                    for j in range(2):
                        for blk in range(2):
                            f = half * BLOCKS + ep * 4 + 2 * j + blk
                            e = ep * 2 + j
                            gv = gm[:, blk, :]
                            dve.wait_ge(f_act, f + 1)
                            v.scalar_tensor_tensor(gv, gv, 1.0, t2[:, blk, :], ALU.add, ALU.mult).then_inc(f_silu, 1)
                            dve.wait_ge(f_silu, f + 1)
                            v.scalar_tensor_tensor(gv, [PJ[1], CS][blk][:], b2t[:, bass.ds(e, 1)], gv, ALU.add,
                                                   ALU.mult).then_inc(f_mul, 1)
                            add_down(f, 1 - blk, e + 1 if blk else e)
                add_down((half + 1) * BLOCKS, 1, SLICES)
                end_phase(dve, half, 2)


_OUT = (HALVES, NT, P, HID)


def kernel(**inputs):
    import concourse.bacc as bacc
    from concourse.bass_utils import run_bass_kernel_spmd

    a = {k: np.asarray(w) for k, w in inputs.items()}
    att = {k[8:]: w for k, w in a.items() if k.startswith("L0_attn_")}
    ffn = {k[7:]: w for k, w in a.items() if k.startswith("L0_ffn_")}

    def by_group(w, n):
        return w.reshape(KV, n, KC, P).transpose(0, 2, 3, 1)

    inv = (np.float32(1.0) / np.float32(10000.0) ** (np.arange(0, D, 2, dtype=np.float32) / np.float32(D)))
    ang = inv.astype(np.float32)[:, None] * np.arange(L, dtype=np.float32)[None, :]
    cos, sin = np.cos(ang).astype(np.float32), np.sin(ang).astype(np.float32)

    def up(we, ws):
        w = np.concatenate([we, ws.reshape(HID, 2, P).transpose(1, 0, 2)])
        return w.reshape(SLICES, KC, P, P).transpose(0, 2, 1, 3).reshape(SLICES, P, HID)

    w3 = np.concatenate([ffn["ew3"], ffn["sw3"].reshape(2, P, HID)])
    arrays = dict(
        x=att["hidden_states"].reshape(HALVES, NT, P, HID),
        wq=by_group(att["Wq"], HG * D),
        wg=by_group(att["Wg"], HG * D),
        wkv=np.concatenate([by_group(att["Wk"], D), by_group(att["Wv"], D)], axis=3)
        .reshape(KV, 2, 2, P, 2 * D).transpose(0, 1, 3, 2, 4).reshape(KV, 2, P, 4 * D),
        wo=att["Wo"].reshape(HID, KV, HG, D).transpose(1, 2, 3, 0),
        wlog=np.concatenate([att["Win"].T, ffn["router_w"]], axis=1).reshape(KC, P, LW).transpose(1, 0, 2),
        dtb=att["dt_bias"], alog=att["A_log_bias"], gnw=att["gnorm_w"].reshape(D, 1),
        rb=ffn["router_b"], rbias=ffn["router_bias"],
        w123=np.concatenate([up(ffn["ew1"], ffn["sw1"]), up(ffn["ew2"], ffn["sw2"]), w3], axis=2),
        b1=np.concatenate([ffn["eb1"], ffn["sb1"].reshape(2, P)]).T,
        b2=np.concatenate([ffn["eb2"], ffn["sb2"].reshape(2, P)]).T,
        b3=np.concatenate([ffn["eb3"], ffn["sb3"].reshape(1, HID)]),
        cos=np.concatenate([cos, cos]), sin=np.concatenate([-sin, sin]),
    )
    nc = bacc.Bacc("TRN2", target_bir_lowering=False, num_devices=1)
    feed, args = {}, {}
    for name, w in arrays.items():
        w = np.ascontiguousarray(w)
        feed[f"in_{name}"] = w
        args[name] = nc.dram_tensor(f"in_{name}", w.shape, mybir.dt.from_np(w.dtype), kind="ExternalInput").ap()
    args["gdram"] = nc.dram_tensor("decay_exponents", (HALVES, H, NT, P), F32, kind="Internal").ap()
    args["out"] = nc.dram_tensor("out", _OUT, F32, kind="ExternalOutput").ap()
    build(nc, **args)
    r = run_bass_kernel_spmd(nc, [feed], core_ids=[0])
    return np.asarray(r.results[0]["out"]).reshape(B, L, HID)
```

```python
from contextlib import ExitStack

import numpy as np

import concourse.bass as bass
from concourse import mybir

F32 = mybir.dt.float32
F32R = mybir.dt.float32r
ALU = mybir.AluOpType
ACT = mybir.ActivationFunctionType
AX = mybir.AxisListType

P = 128
HID = 512
KC = HID // P
H, KV, D = 32, 8, 128
HG = H // KV
B, L = 4, 512
NCH = L // P
HALVES = 2
ROWS = B // HALVES
NT = ROWS * NCH
TOK = NT * P
E, GROUPS = 16, 4
EG = E // GROUPS
SLICES = E + 2
RMS_EPS = 1e-5
LN_EPS = 1e-5
MASKED = -1e30
LW = H + E

STEPS = KV * ROWS
ATT_PIECES = 6 + 14 * KV
FFN_PIECES = 4 * (SLICES + 1)
HALF_PIECES = ATT_PIECES + FFN_PIECES
PW = 3 * 512 // 4
BLOCKS = ROWS * SLICES
XQ = 4
CONSTS = 14
CONST_DMAS = 10


def build(nc, x, order, wq, wg, wkv, wo, wlog, dtb, alog, gnw, rb, rbias, w123, b1, b2, b3, cos, sin, gdram, out):
    ctx = ExitStack()
    with ctx:
        def sb(name, shape, dt=F32):
            return ctx.enter_context(nc.sbuf_tensor(name, shape, dt))

        def pb(name):
            return ctx.enter_context(nc.psum_tensor(name, [P, 512], F32))

        xnh = sb("xnh", [P, KC, TOK], F32R)
        xnl = sb("xnl", [P, KC, TOK], F32R)
        acc = sb("acc", [P, NT, HID])
        coef = sb("coef", [P, 4, NT, H])
        negG = coef[:, 0]
        dt = coef[:, 1]
        wdec = coef[:, 2]
        cdec = coef[:, 3]
        hcoef = sb("hcoef", [P, ROWS, 4, NCH, HG])
        fb1 = sb("fb1", [P, 2])
        gate18 = sb("gate18", [P, NT, SLICES + 1])
        wqh = sb("wqh", [P, KC, 512], F32R)
        wql = sb("wql", [P, KC, 512], F32R)
        wgh = sb("wgh", [P, KC, 512], F32R)
        wgl = sb("wgl", [P, KC, 512], F32R)
        woh = sb("woh", [P, HG, 512], F32R)
        wol = sb("wol", [P, HG, 512], F32R)
        wkvh = sb("wkvh", [P, KC, 256], F32R)
        wkvl = sb("wkvl", [P, KC, 256], F32R)
        stage = sb("stage", [P, 2, 512])
        qh = sb("qh", [P, HG, 512], F32R)
        ql = sb("ql", [P, HG, 512], F32R)
        kh = sb("kh", [P, 512], F32R)
        kl = sb("kl", [P, 512], F32R)
        knh = sb("knh", [P, 3, P], F32R)
        knl = sb("knl", [P, 3, P], F32R)
        vh = sb("vh", [P, 512], F32R)
        vl = sb("vl", [P, 512], F32R)
        vf = sb("vf", [P, 512])
        t1 = sb("t1", [P, 512])
        t2 = sb("t2", [P, 2, 512])
        y2 = sb("y2", [P, 512])
        gate = sb("gate", [P, HG, 512])
        yb = sb("yb", [P, NCH, 512])
        rs = sb("rs", [P, NCH, 512])
        zh = sb("zh", [P, 512], F32R)
        zl = sb("zl", [P, 512], F32R)
        gbc = sb("gbc", [P, 2, 512])
        gm = sb("gm", [P, 2, 512])
        wfh = sb("wfh", [P, 512], F32R)
        wfl = sb("wfl", [P, 512], F32R)
        st = sb("st", [P, 512])
        sth = sb("sth", [P, 512], F32R)
        stl = sb("stl", [P, 512], F32R)
        vwh = sb("vwh", [P, 512], F32R)
        vwl = sb("vwl", [P, 512], F32R)
        cosb = sb("cosb", [P, 512])
        sinb = sb("sinb", [P, 512])
        ones = sb("ones", [P, P])
        ident = sb("ident", [P, P])
        upper = sb("upper", [P, P])
        amask = sb("amask", [P, P])
        onesr = sb("onesr", [P, P], F32R)
        orderb = sb("orderb", [P, E])
        dtbb = sb("dtbb", [P, H])
        nA = sb("nA", [P, H])
        rbb = sb("rbb", [P, E])
        rbiasb = sb("rbiasb", [P, E])
        gn = sb("gn", [P, 1])
        b1t = sb("b1t", [P, SLICES])
        b2t = sb("b2t", [P, SLICES])
        rstd = sb("rstd", [P, NT])
        lneps = sb("lneps", [P, 1])
        rmseps = sb("rmseps", [P, 1])
        one = sb("one", [P, 1])

        gflat = gate[:].rearrange("p a b -> p (a b)")
        rflat = rs[:].rearrange("p a b -> p (a b)")
        yflat = yb[:].rearrange("p a b -> p (a b)")
        gmflat = gm[:].rearrange("p a b -> p (a b)")
        wgfh = wgh[:].rearrange("p a b -> p (a b)")
        wgfl = wgl[:].rearrange("p a b -> p (a b)")
        wqfh = wqh[:].rearrange("p a b -> p (a b)")
        wqfl = wql[:].rearrange("p a b -> p (a b)")
        wlh = wgfh[:, 0:KC * P].rearrange("p (k n) -> p k n", k=KC)
        wll = wgfl[:, 0:KC * P].rearrange("p (k n) -> p k n", k=KC)
        NH8 = NT * H
        lg = gflat[:, 0:NT * LW].rearrange("p (t n) -> p t n", t=NT)

        def small(i):
            o = NT * LW + i * NH8
            return gflat[:, o:o + NH8].rearrange("p (t n) -> p t n", t=NT)

        zz, ee, uu, ll, dd, gg = [small(i) for i in range(6)]
        gcum = t1[:, 0:NH8]
        b3t = vf[0:E + 1, :]
        bst = st[:, 0:6 * NT].rearrange("p (t n) -> p t n", t=NT)
        mv = st[:, 6 * NT:8 * NT].rearrange("p (t n) -> p t n", t=NT)
        wlraw = rflat[:, 0:KC * P].rearrange("p (k n) -> p k n", k=KC)

        def route(o, n):
            return rflat[:, KC * P + o:KC * P + o + NT * n].rearrange("p (t n) -> p t n", t=NT)

        sm, sc_, mk, rk = route(0, E), route(128, E), route(256, E), route(384, E)
        gmx, grk, keep = route(512, GROUPS), route(544, GROUPS), route(576, GROUPS)
        mx1, sum1, rcp1 = route(608, 1), route(616, 1), route(624, 1)
        gw, wk = route(640, GROUPS), route(672, E)
        gT = gmflat[:, 0:2 * P].rearrange("p (a b) -> p a b", a=2)
        logT = t2[:].rearrange("p a b -> p (a b)")
        gateT = t2[0:E + 1].rearrange("p a b -> p (a b)")

        PJ = [pb("PJ0"), pb("PJ1")]
        SC, TR, YI, YE, CS, OU = [pb(n) for n in ("SC", "TR", "YI", "YE", "CS", "OU")]

        B3 = [PJ[0], PJ[1], TR, SC, YI, CS, OU, YE]

        STEP_N = {}

        def step_sem(name, n):
            s_ = ctx.enter_context(nc.semaphore(name))
            STEP_N[name] = (s_, n)
            return s_

        def sem(name):
            return ctx.enter_context(nc.semaphore(name))

        per_step = dict(
            proj=10, tr=2, score=4, cstate=3, yinter=3, yintra=4, ssq=4, oproj=4,
            vraw=1, ropehi=5, vhi=1, knhi=1, dec=4, expg=3, vwhi=3, whi=4, sthi=3, tanh=4, ysq=4, ssqc=4,
            rsln=1, rms=1, zhi=4,
            coef=1, roperd=5, rope=5, knlo=1, wsc=4, wlo=4, vwlo=3, stt=3, stlo=3, yt=3, y=4, gated=4, u=4, z=4, accd=4,
            ropelo=5, vlo=1, gmask=4, zlo=4,
        )
        LAGGED = {"oproj", "rsln", "rms", "zhi", "z", "accd", "zlo"}
        S = {k: sem("s_" + k) for k in per_step}

        const_in = sem("const_in")
        const_made = sem("const_made")
        passed = sem("passed")
        phase = sem("phase")
        x_in = [sem(f"x_in{j}") for j in range(XQ)]
        out_done = sem("out_done")
        wl_in = sem("wl_in")
        stg = [sem("stg0"), sem("stg1")]
        wsplit_hi = sem("wsplit_hi")
        wsplit_lo = sem("wsplit_lo")
        gb_in = [sem("gb_in0"), sem("gb_in1")]
        g_out = sem("g_out")
        dseq = sem("dve_chain")
        aseq = sem("act_chain")
        ln_stats = sem("ln_stats")
        ln_std = sem("ln_std")
        xt_made = sem("xt_made")
        xt_tr = sem("xt_tr")
        xt_hi = sem("xt_hi")
        xt_lo = sem("xt_lo")
        wl_hi = sem("wl_hi")
        wl_lo = sem("wl_lo")
        lt_made = sem("lt_made")
        lt_copied = sem("lt_copied")
        logits = sem("logits")
        to_act = sem("to_act")
        to_dve = sem("to_dve")
        g_made = sem("g_made")
        cums = sem("cums")
        gcum_made = sem("gcum_made")
        gtr = sem("gtr")
        gt_copied = sem("gt_copied")
        gate_made = sem("gate_made")
        gate_tr = sem("gate_tr")
        gateT_made = sem("gateT_made")
        b3_in = sem("b3_in")
        b3_done = sem("b3_done")
        f_up = sem("f_up")
        f_bias = sem("f_bias")
        f_act = sem("f_act")
        f_silu = sem("f_silu")
        f_mul = sem("f_mul")
        f_hi = sem("f_hi")
        f_lo = sem("f_lo")
        f_down = sem("f_down")
        f_acc = sem("f_acc")

        def value(name, s, half, k):
            n = per_step[name]
            if name in LAGGED:
                s = s + half
            return n * (s + 1) + k

        class At:

            def __init__(self, eng, s, half):
                self.eng, self.s, self.half = eng, s, half

            def wait(self, name, k):
                self.put(S[name], value(name, self.s, self.half, k))

            def before(self, name, k):
                self.put(S[name], value(name, self.s, self.half, k - per_step[name]))

            def put(self, semaphore, count):
                if self.eng is nc.sync:
                    hold(self.eng, semaphore, count)
                else:
                    self.eng.wait_ge(semaphore, count)

        def piece_base(half):
            return half * HALF_PIECES

        NPH = 3

        def hold(eng, semaphore, count):
            eng.wait_ge(semaphore, count)
            eng.sem_inc(passed, 1)

        def end_phase(eng, half, k):
            eng.drain().then_inc(phase, 1)
            hold(eng, phase, half * (4 * NPH) + 4 * (k + 2))

        def wkvflat(t, j):
            return t[:, 2 * j:2 * j + 2, :].rearrange("p a b -> p (a b)")

        HH, HL = [vwh, sth], [vwl, stl]
        FW = [(wqfh, wqfl), (wgfh, wgfl)]

        def z_lo(pool, at, c):
            at.wait("zhi", c + 1)
            nc.gpsimd.tensor_tensor(zl[:], yb[:, c, :], zh[:].bitcast(F32), ALU.subtract).then_inc(S["zlo"], 1)

        block = ctx.enter_context(nc.Block())

        @block.sync
        def _(sp):
            for name, n in per_step.items():
                sp.sem_inc(S[name], n)
            sp.sem_inc(wsplit_lo, 2)
            sp.sem_inc(f_mul, 2)
            sp.sem_inc(f_lo, 2)
            sp.sem_inc(f_down, 4)
            sp.sem_inc(phase, 4)
            sp.sem_inc(out_done, 32)
            sp.sem_inc(f_acc, 4)
            def piece(half, n, src):
                hold(sp, wsplit_lo, piece_base(half) + n[0] + 1)
                sp.dma_start(stage[:, n[1], 0:src.shape[-1]], src).then_inc(stg[n[1]], 16)

            with sp.Fori(0, HALVES) as half:
                hold(sp, out_done, (half + 1) * 32)
                xv = x[bass.ds(half, 1), :, :, :].rearrange("o t p n -> p (o t) n")
                for j in range(XQ):
                    ts = slice(j * NT // XQ, (j + 1) * NT // XQ)
                    sp.dma_start(acc[:, ts, :], xv[:, ts, :]).then_inc(x_in[j], 16)
                hold(sp, phase, half * (4 * NPH) + 4)
                sp.wait_ge(const_made, CONSTS)
                sp.dma_start(wlraw, wlog).then_inc(wl_in, 16)
                sp.dma_start(b3t, b3).then_inc(b3_in, 16)
                for j in range(2):
                    piece(half, (j, j % 2), wkv[0, j])
                for j in range(4):
                    piece(half, (2 + j, j % 2), wq[0, j])
                for a in range(2):
                    hold(sp, gt_copied, half * 2 + a + 1)
                    for t in range(4):
                        sp.dma_start(gdram[bass.ds(half, 1), :, 4 * a + t, :].rearrange("o h i -> (o h) i"),
                                     gT[t * H:(t + 1) * H, a, :]).then_inc(g_out, 16)
                hold(sp, g_out, (half + 1) * (16 * 8))
                hold(sp, phase, half * (4 * NPH) + 8)

                with sp.Fori(0, KV) as kv:
                    kvn = (kv + 1) % KV
                    for b in range(ROWS):
                        s = half * STEPS + kv * ROWS + b
                        at = At(sp, s, half)

                        def gload(c):
                            if c < 2:
                                at.before("expg", c + 2)
                                at.before("gmask", c + 3)
                            elif c == 2:
                                at.wait("gmask", 1)
                            else:
                                at.wait("expg", 1)
                                at.wait("gmask", 2)
                            src = gdram[bass.ds(half, 1), bass.ds(kv * HG, HG), b * NCH + c, :]
                            src = src.rearrange("o h i -> (o h) i").partition_broadcast(P)
                            sp.dma_start(gbc[:, c % 2, :].rearrange("p (h i) -> p h i", h=HG), src).then_inc(
                                gb_in[c % 2], 16)

                        def att_piece(j, src):
                            piece(half, (6 + kv * 14 + j, j % 2), src)

                        def row(w, k, j):
                            return w[bass.ds(k, 1), j].rearrange("o p n -> (o p) n")

                        if b == 0:
                            gload(0)
                            att_piece(0, row(wg, kv, 0))
                            att_piece(1, row(wg, kv, 1))
                            gload(1)
                            att_piece(2, row(wg, kv, 2))
                            att_piece(3, row(wg, kv, 3))
                            gload(2)
                            att_piece(4, row(wo, kv, 0))
                            att_piece(5, row(wo, kv, 1))
                            gload(3)
                        else:
                            gload(0)
                            gload(1)
                            att_piece(6, row(wo, kv, 2))
                            att_piece(7, row(wo, kv, 3))
                            gload(2)
                            att_piece(8, row(wkv, kvn, 0))
                            att_piece(9, row(wkv, kvn, 1))
                            gload(3)
                            att_piece(10, row(wq, kvn, 0))
                            att_piece(11, row(wq, kvn, 1))
                            att_piece(12, row(wq, kvn, 2))
                            att_piece(13, row(wq, kvn, 3))
                def ffn_pieces(e, n0):
                    for i in range(4):
                        piece(half, (ATT_PIECES + n0 + i, i % 2),
                              w123[bass.ds(e, 1), :, i * PW:(i + 1) * PW].rearrange("o p n -> (o p) n"))

                ffn_pieces(0, 0)
                with sp.Fori(0, SLICES // 2) as ep:
                    for j in range(2):
                        ffn_pieces((ep * 2 + j + 1) % SLICES, ep * 8 + 4 * j + 4)
                hold(sp, phase, half * (4 * NPH) + 16)
                ov = out[bass.ds(half, 1), :, :, :].rearrange("o t p n -> p (o t) n")
                for j in range(2):
                    sp.dma_start(ov[:, 4 * j:4 * j + 4, :], acc[:, 4 * j:4 * j + 4, :]).then_inc(out_done, 16)
            sp.wait_ge(out_done, (HALVES + 1) * 32)

        @block.gpsimd
        def _(pool):
            g = nc.gpsimd
            made = [0]

            def link(ins):
                made[0] += 1
                ins.then_inc(const_made, 1)
                pool.wait_ge(const_made, made[0])

            for t, v in ((ones, 1.0), (ident, 0.0), (upper, 1.0), (amask, 0.0), (lneps, LN_EPS),
                         (rmseps, RMS_EPS), (one, 1.0), (gate18, 1.0), (rs, 1.0)):
                link(g.memset(t[:], v))
            for t in (woh, wol):
                link(g.memset(t[:].bitcast(F32), 0.0))
            link(g.affine_select(out=ident[:], in_=ident[:], compare_op=ALU.not_equal, fill=1.0, base=0,
                                 pattern=[[-1, P]], channel_multiplier=1))
            link(g.affine_select(out=upper[:], in_=upper[:], compare_op=ALU.is_ge, fill=0.0, base=0,
                                 pattern=[[1, P]], channel_multiplier=-1))
            link(g.affine_select(out=amask[:], in_=amask[:], compare_op=ALU.is_ge, fill=MASKED, base=0,
                                 pattern=[[1, P]], channel_multiplier=-1))

            def split_lo(half, n, hi_out, lo_out):
                pool.wait_ge(wsplit_hi, piece_base(half) + n[0] + 1)
                g.tensor_tensor(lo_out, stage[:, n[1], 0:lo_out.shape[-1]], hi_out.bitcast(F32), ALU.subtract).then_inc(wsplit_lo, 1)

            with pool.Fori(0, HALVES) as half:
                g.memset(yb[:], 0.0)
                for j in range(2):
                    split_lo(half, (j, j % 2), wkvflat(wkvh, j), wkvflat(wkvl, j))
                for j in range(4):
                    split_lo(half, (2 + j, j % 2), wqh[:, j, :], wql[:, j, :])
                hold(pool, gate_made, half + 1)
                g.memset(rs[:], 1.0)
                end_phase(pool, half, 0)
                with pool.Fori(0, KV) as kv:
                    for b in range(ROWS):
                        s = half * STEPS + kv * ROWS + b
                        at = At(pool, s, half)

                        def w_lo(j, hi_out, lo_out):
                            split_lo(half, (6 + kv * 14 + j, j % 2), hi_out, lo_out)

                        def gmasked(c):
                            pool.wait_ge(gb_in[c % 2], (s * 2 + c // 2 + 1) * 16)
                            if c < 2:
                                at.before("wlo", c + 3)
                            else:
                                at.wait("wlo", c - 1)
                            g.tensor_tensor(gm[:, c % 2, :].rearrange("p (h i) -> p h i", h=HG),
                                            gbc[:, c % 2, :].rearrange("p (h i) -> p h i", h=HG),
                                            amask[:].unsqueeze(1).broadcast_to([P, HG, P]),
                                            ALU.add).then_inc(S["gmask"], 1)

                        def rope_lo(i, hi, lo):
                            at.wait("ropehi", i + 1)
                            g.tensor_tensor(lo, t2[:, (5 * b + i) % 2, :], hi.bitcast(F32),
                                            ALU.subtract).then_inc(S["ropelo"], 1)

                        def weight_lo(i):
                            if b == 0:
                                w_lo(i, wgh[:, i, :], wgl[:, i, :])
                            else:
                                w_lo(4 + i, woh[:, i, :], wol[:, i, :])

                        gmasked(0)
                        weight_lo(0)
                        weight_lo(1)
                        rope_lo(0, kh[:], kl[:])
                        at.wait("vhi", 1)
                        g.tensor_tensor(vl[:], vf[:], vh[:].bitcast(F32), ALU.subtract).then_inc(S["vlo"], 1)
                        for j in range(4):
                            if j == 1:
                                weight_lo(3)
                            rope_lo(j + 1, qh[:, j, :], ql[:, j, :])
                            if j == 0:
                                z_lo(pool, at, 0)
                                weight_lo(2)
                            elif j == 2:
                                gmasked(1)
                        for c in range(NCH - 1):
                            z_lo(pool, at, c + 1)
                            if c < 2:
                                gmasked(c + 2)
                            if b == 1:
                                for j in (2 * c, 2 * c + 1):
                                    if j < 2:
                                        w_lo(8 + j, wkvflat(wkvh, j), wkvflat(wkvl, j))
                                    else:
                                        w_lo(8 + j, wqh[:, j - 2, :], wql[:, j - 2, :])
                at = At(pool, half * STEPS + STEPS, half)
                for c in range(NCH):
                    z_lo(pool, at, c)
                end_phase(pool, half, 1)
                def ffn_lo(j, n0, pieces):
                    for i in pieces:
                        o = slice(i * PW, (i + 1) * PW)
                        split_lo(half, (ATT_PIECES + n0 + i, i % 2), FW[j][0][:, o], FW[j][1][:, o])

                ffn_lo(0, 0, (0, 1, 2, 3))
                with pool.Fori(0, SLICES // 2) as ep:
                    for j in range(2):
                        for blk in range(2):
                            f = half * BLOCKS + ep * 4 + 2 * j + blk
                            if blk == 0:
                                ffn_lo(1 - j, ep * 8 + 4 * j + 4, (0, 1))
                            pool.wait_ge(f_hi, f + 1)
                            g.tensor_tensor(HL[blk][:], gm[:, blk, :], HH[blk][:].bitcast(F32),
                                            ALU.subtract).then_inc(f_lo, 1)
                            if blk == 0:
                                ffn_lo(1 - j, ep * 8 + 4 * j + 4, (2, 3))
                end_phase(pool, half, 2)

        @block.scalar
        def _(act):
            a = nc.scalar

            def split_hi(half, n, hi_out):
                act.wait_ge(stg[n[1]], ((piece_base(half) + n[0] - n[1]) // 2 + 1) * 16)
                a.activation(hi_out, stage[:, n[1], 0:hi_out.shape[-1]], ACT.Copy).then_inc(wsplit_hi, 1)

            for dst, src in ((cosb[:], cos), (sinb[:], sin), (dtbb[:], dtb.partition_broadcast(P)),
                             (nA[:], alog.partition_broadcast(P)), (rbb[:], rb.partition_broadcast(P)),
                             (rbiasb[:], rbias.partition_broadcast(P)), (gn[:], gnw), (b1t[:], b1), (b2t[:], b2),
                             (orderb[:], order.partition_broadcast(P))):
                act.dma_start(dst, src).then_inc(const_in, 16)
            act.wait_ge(const_in, 16 * CONST_DMAS)
            act.wait_ge(const_made, CONSTS)
            a.activation(onesr[:], ones[:], ACT.Copy)
            a.activation(gn[:], gn[:], ACT.Copy, scale=0.5).then_inc(aseq, 1)
            a.activation(b1t[:], b1t[:], ACT.Copy, scale=0.5).then_inc(aseq, 1)
            a.activation(nA[:], nA[:], ACT.Exp).then_inc(aseq, 1)
            act.wait_ge(aseq, 3)
            with act.Fori(0, HALVES) as half:
                act.wait_ge(wl_in, (half + 1) * 16)
                a.activation(wlh, wlraw, ACT.Copy).then_inc(wl_hi, 1)
                act.wait_ge(ln_stats, half + 1)
                a.activation(rstd[:], mv[:, :, 1], ACT.Sqrt, bias=lneps[:, 0:1]).then_inc(ln_std, 1)
                for t in range(NT):
                    act.wait_ge(xt_tr, half * NT + t + 1)
                    a.activation(xnh[:, :, t * P:(t + 1) * P], PJ[t % 2][:].rearrange("p (k n) -> p k n", k=KC),
                                 ACT.Copy).then_inc(xt_hi, 1)
                for j in range(2):
                    split_hi(half, (j, j % 2), wkvflat(wkvh, j))
                for j in range(4):
                    split_hi(half, (2 + j, j % 2), wqh[:, j, :])
                act.wait_ge(to_act, half * 4 + 1)
                a.activation(sm, sm, ACT.Exp).then_inc(to_dve, 1)
                act.wait_ge(to_act, half * 4 + 2)
                a.activation(ee, ee, ACT.Exp, scale=-1.0).then_inc(to_dve, 1)
                act.wait_ge(to_act, half * 4 + 3)
                a.activation(ll, uu, ACT.Ln).then_inc(to_dve, 1)
                act.wait_ge(to_act, half * 4 + 4)
                a.activation(wdec, wdec, ACT.Exp).then_inc(to_dve, 1)
                a.activation(cdec, cdec, ACT.Exp).then_inc(to_dve, 1)
                end_phase(act, half, 0)

                def rms_batch(at, half):
                    at.before("ssqc", 4)
                    a.activation(rs[:], rs[:], ACT.Ln, scale=1.0 / D, bias=rmseps[:, 0:1]).then_inc(S["rsln"], 1)
                    at.wait("rsln", 1)
                    a.activation(rs[:], rs[:], ACT.Exp, scale=-0.5).then_inc(S["rms"], 1)

                def z_hi(at, c):
                    at.wait("z", c + 1)
                    if c == 0:
                        at.before("oproj", 4)
                    else:
                        at.wait("oproj", c)
                    a.activation(zh[:], yb[:, c, :], ACT.Copy).then_inc(S["zhi"], 1)

                with act.Fori(0, KV) as kv:
                    for b in range(ROWS):
                        s = half * STEPS + kv * ROWS + b
                        at = At(act, s, half)

                        def w_hi(j, hi_out):
                            split_hi(half, (6 + kv * 14 + j, j % 2), hi_out)

                        def head(kind, c, h):
                            return hcoef[:, b, kind, c, h:h + 1]

                        def rope_hi(i, hi):
                            at.wait("rope", i + 1)
                            a.activation(hi, t2[:, (5 * b + i) % 2, :], ACT.Copy).then_inc(S["ropehi"], 1)

                        def decay(c):
                            at.wait("gmask", c + 1)
                            for h in range(HG):
                                gv = gm[:, c % 2, h * P:(h + 1) * P]
                                ins = a.activation(gv, gv, ACT.Exp, bias=head(0, c, h))
                            ins.then_inc(S["dec"], 1)

                        def exp_g(c):
                            at.wait("zlo", c + 1)
                            a.activation(yb[:, c, :], gbc[:, c % 2, :], ACT.Exp).then_inc(S["expg"], 1)

                        def vw_hi(c):
                            if c:
                                at.wait("cstate", c)
                            else:
                                at.wait("vhi", 1)
                            for h in range(HG):
                                ins = a.activation(vwh[:, h * P:(h + 1) * P], vf[:, c * P:(c + 1) * P], ACT.Copy,
                                                   scale=head(2, c, h))
                            ins.then_inc(S["vwhi"], 1)

                        def weight_hi(i):
                            if b == 0:
                                w_hi(i, wgh[:, i, :])
                            else:
                                w_hi(4 + i, woh[:, i, :])

                        def silu_gate(c):
                            at.wait("proj", 7 + c)
                            if c == 0:
                                at.before("u", 4)
                            a.activation(gate[:, c, :], PJ[c % 2][:], ACT.Tanh, scale=0.5).then_inc(S["tanh"], 1)

                        if b == 0:
                            at.before("proj", 10)
                        else:
                            at.before("oproj", 4)
                        weight_hi(0)
                        weight_hi(1)
                        rms_batch(at, half)
                        rope_hi(0, kh[:])
                        at.wait("tr", 1)
                        a.activation(vf[:], TR[:], ACT.Copy)
                        a.activation(vh[:], TR[:], ACT.Copy).then_inc(S["vhi"], 1)
                        rope_hi(1, qh[:, 0, :])
                        z_hi(at, 0)
                        weight_hi(2)
                        at.wait("coef", 1)
                        vw_hi(0)
                        at.wait("tr", 2)
                        a.activation(knh[:], TR[:, 0:3 * P].rearrange("p (a b) -> p a b", a=3),
                                     ACT.Copy).then_inc(S["knhi"], 1)
                        weight_hi(3)
                        rope_hi(2, qh[:, 1, :])
                        decay(0)
                        rope_hi(3, qh[:, 2, :])
                        rope_hi(4, qh[:, 3, :])
                        z_hi(at, 1)
                        silu_gate(0)
                        for c in range(NCH):
                            at.wait("wsc", c + 1)
                            if c:
                                at.wait("yintra", c)
                            a.activation(wfh[:], gm[:, c % 2, :], ACT.Copy).then_inc(S["whi"], 1)
                            if c < 3:
                                if c < 2:
                                    vw_hi(c + 1)
                                if c:
                                    z_hi(at, c + 1)
                                decay(c + 1)
                                at.wait("stt", c + 1)
                                if c:
                                    at.wait("yinter", c)
                                a.activation(sth[:], st[:], ACT.Copy).then_inc(S["sthi"], 1)
                                if b == 1:
                                    for j in (2 * c, 2 * c + 1):
                                        w_hi(8 + j, wkvflat(wkvh, j) if j < 2 else wqh[:, j - 2, :])
                                silu_gate(c + 1)
                                exp_g(c + 1)
                            if c:
                                at.wait("ssq", c)
                                a.activation(rs[:, c - 1, :], TR[:], ACT.Copy).then_inc(S["ssqc"], 1)
                            at.wait("y", c + 1)
                            a.activation(y2[:], yb[:, c, :], ACT.Square).then_inc(S["ysq"], 1)
                        at.wait("ssq", 4)
                        a.activation(rs[:, 3, :], TR[:], ACT.Copy).then_inc(S["ssqc"], 1)
                at = At(act, half * STEPS + STEPS, half)
                rms_batch(at, half)
                for c in range(NCH):
                    z_hi(at, c)
                end_phase(act, half, 1)

                def ffn_hi(j, n0, pieces):
                    for i in pieces:
                        split_hi(half, (ATT_PIECES + n0 + i, i % 2), FW[j][0][:, i * PW:(i + 1) * PW])

                ffn_hi(0, 0, (0, 1, 2, 3))
                with act.Fori(0, SLICES // 2) as ep:
                    for j in range(2):
                        for blk in range(2):
                            f = half * BLOCKS + ep * 4 + 2 * j + blk
                            bias = fb1[:, j:j + 1]
                            up = [PJ[0], TR][blk]
                            act.wait_ge(f_up, f + 1)
                            act.wait_ge(f_bias, half * (SLICES // 2) + ep + 1)
                            act.wait_ge(f_lo, f + 1)
                            a.activation(t2[:, blk, :], up[:], ACT.Identity, scale=0.5, bias=bias)
                            a.activation(gm[:, blk, :], up[:], ACT.Tanh, scale=0.5, bias=bias).then_inc(f_act, 1)
                            if blk == 0:
                                ffn_hi(1 - j, ep * 8 + 4 * j + 4, (0, 1))
                            act.wait_ge(f_mul, f + 3)
                            act.wait_ge(f_down, (f + half) * 4 + 4)
                            a.activation(HH[blk][:], gm[:, blk, :], ACT.Copy).then_inc(f_hi, 1)
                            if blk == 0:
                                act.wait_ge(f_down, (f + half) * 4 + 8)
                                ffn_hi(1 - j, ep * 8 + 4 * j + 4, (2, 3))
                end_phase(act, half, 2)

        @block.tensor
        def _(pe):
            def mm3(out_, a_hi, a_lo, b_hi, b_lo, first, last):
                nc.tensor.matmul(out_, a_hi, b_hi, start=first, stop=False)
                nc.tensor.matmul(out_, a_hi, b_lo, start=False, stop=False)
                return nc.tensor.matmul(out_, a_lo, b_hi, start=False, stop=last)

            pe.wait_ge(const_made, CONSTS)
            pe.wait_ge(const_in, 16 * CONST_DMAS)
            with pe.Fori(0, HALVES) as half:
                def row_logits(r):
                    pe.wait_ge(wl_lo, half + 1)
                    pe.wait_ge(xt_lo, half * NT + (r + 1) * NCH)
                    rows = slice(r * L, (r + 1) * L)
                    for k in range(KC):
                        ins = mm3((SC, YI)[r][:], wlh[:, k, :], wll[:, k, :], xnh[:, k, rows], xnl[:, k, rows], k == 0,
                                  k == KC - 1)
                    ins.then_inc(lt_made, 1)

                for t in range(NT):
                    if t == NT - 2:
                        row_logits(0)
                    pe.wait_ge(xt_made, half * NT + t + 1)
                    if t >= 2:
                        pe.wait_ge(xt_lo, half * NT + t - 1)
                    for k in range(KC):
                        ins = nc.tensor.transpose(PJ[t % 2][:, k * P:(k + 1) * P], t2[:, t % 2, k * P:(k + 1) * P],
                                                  ident[:])
                    ins.then_inc(xt_tr, 1)
                row_logits(1)
                pe.wait_ge(lt_copied, half + 1)
                for t in range(NT):
                    ins = nc.tensor.transpose((CS, OU)[t // 4][:, t % 4 * P:(t % 4 + 1) * P],
                                              logT[:, t * P:(t + 1) * P], ident[:])
                ins.then_inc(logits, 1)
                pe.wait_ge(g_made, half + 1)
                nc.tensor.matmul(SC[:, 0:NH8], upper[:], gg.rearrange("p t n -> p (t n)"), start=True, stop=True)
                nc.tensor.matmul(YI[:, 0:NH8], ones[:], gg.rearrange("p t n -> p (t n)"), start=True,
                                 stop=True).then_inc(cums, 1)
                pe.wait_ge(gcum_made, half + 1)
                for i in range(2):
                    ins = nc.tensor.transpose(YE[:, i * P:(i + 1) * P], gcum[:, i * P:(i + 1) * P], ident[:])
                ins.then_inc(gtr, 1)
                pe.wait_ge(gate_made, half + 1)
                pe.wait_ge(b3_in, (half + 1) * 16)
                for t in range(NT):
                    bank = (OU, YE)[t // 4]
                    ins = nc.tensor.transpose(bank[0:E + 1, t % 4 * P:(t % 4 + 1) * P], gate18[:, t, 1:E + 2], ident[:])
                ins.then_inc(gate_tr, 1)
                pe.wait_ge(gateT_made, half + 1)
                for t in range(NT):
                    nc.tensor.matmul(B3[t][:], gateT[:, t * P:(t + 1) * P], b3t, start=True, stop=True).then_inc(b3_done, 1)
                end_phase(pe, half, 0)

                def out_proj(at, c, heads=range(HG)):
                    if heads[0] == 0:
                        at.wait("zlo", c + 1)
                        if c == 0:
                            at.before("accd", 4)
                        else:
                            at.wait("accd", c)
                    for h in heads:
                        hs = slice(h * P, (h + 1) * P)
                        ins = mm3(OU[:], zh[:, hs], zl[:, hs], woh[:, h, :], wol[:, h, :], h == 0, h == HG - 1)
                    if heads[-1] == HG - 1:
                        ins.then_inc(S["oproj"], 1)

                with pe.Fori(0, KV) as kv:
                    for b in range(ROWS):
                        s = half * STEPS + kv * ROWS + b
                        at = At(pe, s, half)
                        rows = slice(b * L, (b + 1) * L)

                        def weights(n):
                            pe.wait_ge(wsplit_lo, piece_base(half) + kv * 14 + 6 + n + 2)

                        def project(bank, wh_, wl_):
                            for k in range(KC):
                                ins = mm3(PJ[bank][:], wh_[k], wl_[k], xnh[:, k, rows], xnl[:, k, rows], k == 0,
                                          k == KC - 1)
                            ins.then_inc(S["proj"], 1)

                        def proj_q(j):
                            hs = slice(j * P, (j + 1) * P)
                            project(j % 2, [wqh[:, k, hs] for k in range(KC)], [wql[:, k, hs] for k in range(KC)])

                        def proj_g(j):
                            hs = slice(j * P, (j + 1) * P)
                            project(j % 2, [wgh[:, k, hs] for k in range(KC)], [wgl[:, k, hs] for k in range(KC)])

                        def scores(c):
                            if c == 0:
                                at.before("wsc", 4)
                            else:
                                at.wait("wsc", c)
                            cs = slice(c * P, (c + 1) * P)
                            mm3(SC[:].rearrange("p (h i) -> p h i", h=HG), kh[:, cs], kl[:, cs], qh[:, :, cs],
                                ql[:, :, cs], True, True).then_inc(S["score"], 1)

                        def chunk_state(c):
                            at.wait("vwlo", c + 1)
                            if c == 0:
                                at.wait("knlo", 1)
                                at.before("stt", 3)
                            else:
                                at.wait("stt", c)
                            mm3(CS[:], knh[:, c, :], knl[:, c, :], vwh[:], vwl[:], True, True).then_inc(S["cstate"], 1)

                        def inter(c):
                            at.wait("stlo", c)
                            if c == 1:
                                at.before("yt", 3)
                            else:
                                at.wait("yt", c - 1)
                            cs = slice(c * P, (c + 1) * P)
                            for h in range(HG):
                                hs = slice(h * P, (h + 1) * P)
                                ins = mm3(YE[:, hs], sth[:, hs], stl[:, hs], qh[:, h, cs], ql[:, h, cs], True, True)
                            ins.then_inc(S["yinter"], 1)

                        def intra(c):
                            at.wait("wlo", c + 1)
                            if c == 0:
                                at.wait("vlo", 1)
                                at.before("y", 4)
                            else:
                                at.wait("y", c)
                            cs = slice(c * P, (c + 1) * P)
                            mm3(YI[:], vh[:, cs], vl[:, cs], wfh[:], wfl[:], True, True).then_inc(S["yintra"], 1)

                        def squares(c):
                            at.wait("ysq", c + 1)
                            if c:
                                at.wait("ssqc", c)
                            nc.tensor.matmul(TR[:], ones[:], y2[:], start=True, stop=True).then_inc(S["ssq"], 1)

                        if b == 0:
                            weights(-4)
                        at.before("gated", 3)
                        project(0, [wkvh[:, k, 0:P] for k in range(KC)], [wkvl[:, k, 0:P] for k in range(KC)])
                        at.before("gated", 4)
                        project(1, [wkvh[:, k, P:2 * P] for k in range(KC)], [wkvl[:, k, P:2 * P] for k in range(KC)])
                        if b == 0:
                            weights(0)
                        at.wait("roperd", 1)
                        proj_q(0)
                        at.wait("vraw", 1)
                        at.before("ssqc", 4)
                        for i in range(4):
                            ins = nc.tensor.transpose(TR[:, i * P:(i + 1) * P], y2[:, i * P:(i + 1) * P], ident[:])
                        ins.then_inc(S["tr"], 1)
                        proj_q(1)
                        at.wait("rope", 1)
                        at.wait("vhi", 1)
                        for i in range(3):
                            ins = nc.tensor.transpose(TR[:, i * P:(i + 1) * P], t2[:, (5 * b) % 2, i * P:(i + 1) * P],
                                                      ident[:])
                        ins.then_inc(S["tr"], 1)
                        for j in (2, 3):
                            at.wait("roperd", j)
                            proj_q(j)
                        if b == 1:
                            weights(8)
                        out_proj(at, 0)
                        if b == 0:
                            weights(4)
                        at.wait("roperd", 4)
                        proj_g(0)
                        at.wait("ropelo", 5)
                        scores(0)
                        for c in range(NCH):
                            if c < 3:
                                chunk_state(c)
                            if c:
                                inter(c)
                            if c < 3:
                                if c == 0:
                                    at.wait("roperd", 5)
                                else:
                                    at.wait("gated", c)
                                proj_g(c + 1)
                            intra(c)
                            if c < 3:
                                scores(c + 1)
                            if c:
                                squares(c - 1)
                            if c < 2:
                                out_proj(at, c + 1)
                            elif c == 2:
                                out_proj(at, 3, range(HG // 2))
                        out_proj(at, 3, range(HG // 2, HG))
                        squares(3)
                at = At(pe, half * STEPS + STEPS, half)
                for c in range(NCH):
                    out_proj(at, c)
                end_phase(pe, half, 1)

                def down(f, blk, j):
                    pe.wait_ge(f_lo, f + 2)
                    for t, bank in enumerate((SC, YI, YE, OU)):
                        ts = slice(t * P, (t + 1) * P)
                        pe.wait_ge(f_acc, (f + half) * 4 + t + 1)
                        mm3(bank[:], HH[blk][:, ts], HL[blk][:, ts], FW[j][0][:, 1024:1536], FW[j][1][:, 1024:1536],
                            True, True).then_inc(f_down, 1)

                with pe.Fori(0, SLICES // 2) as ep:
                    for j in range(2):
                        pe.wait_ge(wsplit_lo, piece_base(half) + ATT_PIECES + ep * 8 + 4 * j + 4 + 2)
                        for blk in range(2):
                            f = half * BLOCKS + ep * 4 + 2 * j + blk
                            pe.wait_ge(f_mul, f + 1)
                            rows = slice(blk * L, (blk + 1) * L)
                            for i, bank in enumerate(([PJ[0], PJ[1]], [TR, CS])[blk]):
                                for k in range(KC):
                                    ws = slice(i * 512 + k * P, i * 512 + (k + 1) * P)
                                    ins = mm3(bank[:], FW[j][0][:, ws], FW[j][1][:, ws], xnh[:, k, rows],
                                              xnl[:, k, rows], k == 0, k == KC - 1)
                            ins.then_inc(f_up, 1)
                            down(f, 1 - blk, j if blk else 1 - j)
                down((half + 1) * BLOCKS, 1, 1)
                end_phase(pe, half, 2)

        @block.vector
        def _(dve):
            v = nc.vector
            PRO = 80
            dve.wait_ge(const_made, CONSTS)
            dve.wait_ge(const_in, 16 * CONST_DMAS)
            with dve.Fori(0, HALVES) as half:
                n = [0]

                def link(ins):
                    n[0] += 1
                    ins.then_inc(dseq, 1)
                    dve.wait_ge(dseq, half * PRO + n[0])

                for t in range(NT):
                    if t % (NT // XQ) == 0:
                        dve.wait_ge(x_in[t * XQ // NT], (half + 1) * 16)
                    ins = v.bn_stats(bst[:, t, :], acc[:, t, :])
                link(ins)
                v.memset(gate18[:, :, 0], 0.0)
                for t in range(NT):
                    ins = v.bn_aggr(mv[:, t, :], bst[:, t, :])
                ins.then_inc(ln_stats, 1)
                dve.wait_ge(ln_std, half + 1)
                link(v.reciprocal(rstd[:], rstd[:]))

                def normalise(t):
                    if t >= 2:
                        dve.wait_ge(xt_tr, half * NT + t - 1)
                    v.tensor_scalar(t2[:, t % 2, :], acc[:, t, :], mv[:, t, 0:1], rstd[:, t:t + 1], ALU.subtract,
                                    ALU.mult).then_inc(xt_made, 1)

                normalise(0)
                for t in range(NT):
                    if t + 1 < NT:
                        normalise(t + 1)
                    dve.wait_ge(xt_hi, half * NT + t + 1)
                    ts = slice(t * P, (t + 1) * P)
                    v.tensor_tensor(xnl[:, :, ts], PJ[t % 2][:].rearrange("p (k n) -> p k n", k=KC),
                                    xnh[:, :, ts].bitcast(F32), ALU.subtract).then_inc(xt_lo, 1)
                    if t == 0:
                        dve.wait_ge(wl_hi, half + 1)
                        v.tensor_tensor(wll, wlraw, wlh.bitcast(F32), ALU.subtract).then_inc(wl_lo, 1)

                def bc(ap, shape, axis):
                    return ap.unsqueeze(axis).broadcast_to(shape)

                for r in range(2):
                    dve.wait_ge(lt_made, half * 2 + r + 1)
                    ins = v.tensor_copy(logT[:, r * L:(r + 1) * L], (SC, YI)[r][:])
                ins.then_inc(lt_copied, 1)
                dve.wait_ge(logits, half + 1)
                for r, bank in enumerate((CS, OU)):
                    ins = v.tensor_copy(lg[:, r * NCH:(r + 1) * NCH, :],
                                        bank[:].rearrange("p (t n) -> p t n", t=NCH)[:, :, 0:LW])
                link(ins)
                lgr = lg[:, :, H:LW]
                link(v.tensor_tensor(lgr, lgr, bc(rbb[:], [P, NT, E], 1), ALU.add))
                link(v.tensor_reduce(mx1[:, :, 0], lgr, AX.X, ALU.max))
                v.tensor_tensor(sm, lgr, mx1.broadcast_to([P, NT, E]), ALU.subtract).then_inc(to_act, 1)
                link(v.tensor_tensor(zz, lg[:, :, 0:H], bc(dtbb[:], [P, NT, H], 1), ALU.add))
                link(v.tensor_scalar(dd, zz, -1.0, None, ALU.mult))
                v.tensor_tensor(ee, zz, dd, ALU.max).then_inc(to_act, 1)
                dve.wait_ge(to_dve, half * 5 + 2)
                link(v.tensor_scalar(uu, ee, 1.0, None, ALU.add))
                v.tensor_scalar(dd, uu, 1.0, None, ALU.subtract).then_inc(to_act, 1)
                dve.wait_ge(to_dve, half * 5 + 3)
                link(v.tensor_scalar(gg, dd, 0.0, None, ALU.is_equal))
                link(v.tensor_tensor(ll, ll, gg, ALU.add))
                link(v.tensor_tensor(dd, dd, gg, ALU.add))
                link(v.tensor_tensor(ll, ll, ee, ALU.mult))
                link(v.reciprocal(dd, dd))
                link(v.tensor_tensor(ll, ll, dd, ALU.mult))
                link(v.scalar_tensor_tensor(dt, zz, 0.0, ll, ALU.max, ALU.add))
                link(v.tensor_tensor(gg, dt, bc(nA[:], [P, NT, H], 1), ALU.mult))
                v.tensor_scalar(gg, gg, -1.0, None, ALU.mult).then_inc(g_made, 1)
                dve.wait_ge(cums, half + 1)
                link(v.tensor_copy(gcum, SC[:, 0:NH8]))
                gc3 = gcum.rearrange("p (t n) -> p t n", t=NT)
                last3 = YI[:, 0:NH8].rearrange("p (t n) -> p t n", t=NT)
                v.tensor_scalar(negG, gc3, -1.0, None, ALU.mult).then_inc(gcum_made, 1)
                v.tensor_tensor(wdec, last3, gc3, ALU.subtract)
                v.tensor_copy(cdec, last3).then_inc(to_act, 1)
                for i in range(2):
                    if i == 0:
                        dve.wait_ge(gtr, half + 1)
                    v.tensor_copy(gT[:, i, :], YE[:, i * P:(i + 1) * P]).then_inc(gt_copied, 1)

                link(v.tensor_reduce(sum1[:, :, 0], sm, AX.X, ALU.add))
                link(v.reciprocal(rcp1, sum1))
                link(v.tensor_tensor(sc_, sm, rcp1.broadcast_to([P, NT, E]), ALU.mult))
                link(v.tensor_tensor(sc_, sc_, bc(rbiasb[:], [P, NT, E], 1), ALU.add))

                def best_two(out_, vals, m, work):
                    shape = [P, NT, m]
                    first, rest = work
                    left = vals
                    for i in range(2):
                        link(v.tensor_reduce(mx1[:, :, 0], left, AX.X, ALU.max))
                        link(v.tensor_tensor(first, left, mx1.broadcast_to(shape), ALU.is_equal))
                        link(v.tensor_tensor(first, first, bc(orderb[:, 0:m], shape, 1), ALU.mult))
                        link(v.tensor_reduce(mx1[:, :, 0], first, AX.X, ALU.max))
                        link(v.tensor_tensor(first if i else out_, first, mx1.broadcast_to(shape), ALU.is_equal))
                        if i == 0:
                            link(v.scalar_tensor_tensor(rest, out_, MASKED, vals, ALU.mult, ALU.add))
                            left = rest
                    link(v.tensor_tensor(out_, out_, first, ALU.add))

                link(v.tensor_reduce(gmx, sc_.rearrange("p t (g e) -> p t g e", g=GROUPS), AX.X, ALU.max))
                best_two(keep, gmx, GROUPS, (grk, gw))
                link(v.tensor_scalar(keep, keep, -MASKED, MASKED, ALU.mult, ALU.add))
                link(v.tensor_tensor(mk.rearrange("p t (g e) -> p t g e", g=GROUPS),
                                     sc_.rearrange("p t (g e) -> p t g e", g=GROUPS),
                                     bc(keep, [P, NT, GROUPS, EG], 3), ALU.add))
                best_two(rk, mk, E, (sm, wk))
                v.tensor_tensor(gate18[:, :, 1:E + 1], rk, sc_, ALU.mult).then_inc(gate_made, 1)
                dve.wait_ge(to_dve, half * 5 + 5)
                v.tensor_tensor(wdec, wdec, dt, ALU.mult)
                dve.wait_ge(gate_tr, half + 1)
                for i, bank in enumerate((OU, YE)):
                    ins = v.tensor_copy(gateT[:, i * 4 * P:(i + 1) * 4 * P], bank[0:E + 1, :])
                ins.then_inc(gateT_made, 1)
                for t in range(NT):
                    dve.wait_ge(b3_done, half * NT + t + 1)
                    v.tensor_tensor(acc[:, t, :], acc[:, t, :], B3[t][:], ALU.add)
                assert n[0] <= PRO
                dve.sem_inc(dseq, PRO - n[0])
                end_phase(dve, half, 0)

                def late_z(at, c):
                    at.wait("rms", 1)
                    at.before("u", c + 1)
                    v.scalar_tensor_tensor(yb[:, c, :], yb[:, c, :], gn[:, 0:1], rs[:, c, :], ALU.mult,
                                           ALU.mult).then_inc(S["z"], 1)

                def late_acc(at, c, row):
                    at.wait("oproj", c + 1)
                    tile = acc[:, row * NCH + c, :]
                    v.tensor_tensor(tile, tile, OU[:], ALU.add).then_inc(S["accd"], 1)

                with dve.Fori(0, KV) as kv:
                    for b in range(ROWS):
                        s = half * STEPS + kv * ROWS + b
                        at = At(dve, s, half)

                        def head(kind, c, h):
                            return hcoef[:, b, kind, c, h:h + 1]

                        def rope(i, bank):
                            slot = (5 * b + i) % 2
                            at.wait("proj", (1, 3, 4, 5, 6)[i])
                            if i < 2:
                                at.before("ropelo", 4 + i)
                            else:
                                at.wait("ropelo", i - 1)
                            if i == 2:
                                at.wait("tr", 2)
                            if i:
                                at.wait("rope", i)
                            else:
                                at.before("rope", 5)
                            hd = D // 2
                            v.tensor_tensor(t1[:], PJ[bank][:], cosb[:], ALU.mult)
                            v.tensor_tensor(t2[0:hd, slot, :], PJ[bank][hd:D, :], sinb[0:hd, :], ALU.mult)
                            v.tensor_tensor(t2[hd:D, slot, :], PJ[bank][0:hd, :], sinb[hd:D, :],
                                            ALU.mult).then_inc(S["roperd"], 1)
                            at.wait("roperd", i + 1)
                            v.tensor_tensor(t2[:, slot, :], t1[:], t2[:, slot, :], ALU.add).then_inc(S["rope"], 1)

                        def weigh(c):
                            at.wait("score", c + 1)
                            at.wait("dec", c + 1)
                            for h in range(HG):
                                hs = slice(h * P, (h + 1) * P)
                                ins = v.scalar_tensor_tensor(gm[:, c % 2, hs], SC[:, hs], head(1, c, h),
                                                             gm[:, c % 2, hs], ALU.mult, ALU.mult)
                            ins.then_inc(S["wsc"], 1)

                        def vw_lo(c):
                            at.wait("vwhi", c + 1)
                            for h in range(HG):
                                hs = slice(h * P, (h + 1) * P)
                                ins = v.scalar_tensor_tensor(vwl[:, hs], vf[:, c * P:(c + 1) * P], head(2, c, h),
                                                             vwh[:, hs].bitcast(F32), ALU.mult, ALU.subtract)
                            ins.then_inc(S["vwlo"], 1)

                        v.tensor_copy(hcoef[:, b], coef[:, :, b * NCH:(b + 1) * NCH, bass.ds(kv * HG, HG)]).then_inc(
                            S["coef"], 1)
                        at.wait("coef", 1)
                        def gated(c):
                            at.wait("tanh", c + 1)
                            v.scalar_tensor_tensor(gate[:, c, :], gate[:, c, :], 1.0, PJ[c % 2][:], ALU.add,
                                                   ALU.mult).then_inc(S["gated"], 1)

                        rope(0, 0)
                        at.wait("proj", 2)
                        at.before("ssq", 4)
                        v.tensor_copy(y2[:], PJ[1][:]).then_inc(S["vraw"], 1)
                        rope(1, 0)
                        late_z(at, 0)
                        rope(2, 1)
                        rope(3, 0)
                        rope(4, 1)
                        vw_lo(0)
                        at.wait("knhi", 1)
                        v.tensor_tensor(knl[:], TR[:, 0:3 * P].rearrange("p (a b) -> p a b", a=3),
                                        knh[:].bitcast(F32), ALU.subtract).then_inc(S["knlo"], 1)
                        late_z(at, 1)
                        gated(0)
                        weigh(0)
                        for c in range(NCH):
                            if 0 < c < 3:
                                late_z(at, c + 1)
                            at.wait("whi", c + 1)
                            v.tensor_tensor(wfl[:], gm[:, c % 2, :], wfh[:].bitcast(F32),
                                            ALU.subtract).then_inc(S["wlo"], 1)
                            if c < 3:
                                late_acc(at, c, 1 - b)
                                if c < 2:
                                    vw_lo(c + 1)
                            if c < 3:
                                at.wait("cstate", c + 1)
                                if c == 0:
                                    v.tensor_copy(st[:], CS[:]).then_inc(S["stt"], 1)
                                else:
                                    at.wait("sthi", c)
                                    at.wait("stt", c)
                                    for h in range(HG):
                                        hs = slice(h * P, (h + 1) * P)
                                        ins = v.scalar_tensor_tensor(st[:, hs], st[:, hs], head(3, c, h),
                                                                     CS[:, hs], ALU.mult, ALU.add)
                                    ins.then_inc(S["stt"], 1)
                            if c:
                                at.wait("yinter", c)
                                at.wait("expg", c)
                                v.tensor_tensor(yb[:, c, :], YE[:], yb[:, c, :], ALU.mult).then_inc(S["yt"], 1)
                            if c < 3:
                                at.wait("sthi", c + 1)
                                v.tensor_tensor(stl[:], st[:], sth[:].bitcast(F32), ALU.subtract).then_inc(
                                    S["stlo"], 1)
                            at.wait("yintra", c + 1)
                            if c:
                                at.wait("yt", c)
                                v.tensor_tensor(yb[:, c, :], YI[:], yb[:, c, :], ALU.add).then_inc(S["y"], 1)
                            else:
                                at.wait("zlo", 1)
                                v.tensor_copy(yb[:, 0, :], YI[:]).then_inc(S["y"], 1)
                            if c < 3:
                                weigh(c + 1)
                                gated(c + 1)
                        for c in range(NCH):
                            at.wait("ysq", c + 1)
                            if c == 0:
                                at.wait("gated", 4)
                            if c == 3:
                                late_acc(at, 3, 1 - b)
                            yv = yb[:, c, :].rearrange("p (h i) -> p h i", h=HG)
                            v.tensor_tensor(yv, yv, gate[:, :, c * P:(c + 1) * P], ALU.mult).then_inc(S["u"], 1)
                at = At(dve, half * STEPS + STEPS, half)
                for c in range(NCH):
                    late_z(at, c)
                for c in range(NCH):
                    late_acc(at, c, 1)
                end_phase(dve, half, 1)

                def add_down(f, blk, col):
                    for t, bank in enumerate((SC, YI, YE, OU)):
                        dve.wait_ge(f_down, (f + half) * 4 + t + 5)
                        tile = acc[:, blk * NCH + t, :]
                        v.scalar_tensor_tensor(tile, bank[:], gate18[:, blk * NCH + t, bass.ds(col, 1)], tile,
                                               ALU.mult, ALU.add).then_inc(f_acc, 1)

                with dve.Fori(0, SLICES // 2) as ep:
                    v.tensor_copy(fb1[:], b1t[:, bass.ds(ep * 2, 2)]).then_inc(f_bias, 1)
                    for j in range(2):
                        for blk in range(2):
                            f = half * BLOCKS + ep * 4 + 2 * j + blk
                            e = ep * 2 + j
                            gv = gm[:, blk, :]
                            dve.wait_ge(f_act, f + 1)
                            v.scalar_tensor_tensor(gv, gv, 1.0, t2[:, blk, :], ALU.add, ALU.mult).then_inc(f_silu, 1)
                            dve.wait_ge(f_silu, f + 1)
                            v.scalar_tensor_tensor(gv, [PJ[1], CS][blk][:], b2t[:, bass.ds(e, 1)], gv, ALU.add,
                                                   ALU.mult).then_inc(f_mul, 1)
                            add_down(f, 1 - blk, e + 1 if blk else e)
                add_down((half + 1) * BLOCKS, 1, SLICES)
                end_phase(dve, half, 2)


_OUT = (HALVES, NT, P, HID)


def kernel(**inputs):
    import concourse.bacc as bacc
    from concourse.bass_utils import run_bass_kernel_spmd

    a = {k: np.asarray(w) for k, w in inputs.items()}
    att = {k[8:]: w for k, w in a.items() if k.startswith("L0_attn_")}
    ffn = {k[7:]: w for k, w in a.items() if k.startswith("L0_ffn_")}

    def by_group(w, n):
        return w.reshape(KV, n, KC, P).transpose(0, 2, 3, 1)

    inv = (np.float32(1.0) / np.float32(10000.0) ** (np.arange(0, D, 2, dtype=np.float32) / np.float32(D)))
    ang = inv.astype(np.float32)[:, None] * np.arange(L, dtype=np.float32)[None, :]
    cos, sin = np.cos(ang).astype(np.float32), np.sin(ang).astype(np.float32)

    def up(we, ws):
        w = np.concatenate([we, ws.reshape(HID, 2, P).transpose(1, 0, 2)])
        return w.reshape(SLICES, KC, P, P).transpose(0, 2, 1, 3).reshape(SLICES, P, HID)

    w3 = np.concatenate([ffn["ew3"], ffn["sw3"].reshape(2, P, HID)])
    arrays = dict(
        x=att["hidden_states"].reshape(HALVES, NT, P, HID),
        wq=by_group(att["Wq"], HG * D),
        wg=by_group(att["Wg"], HG * D),
        wkv=np.concatenate([by_group(att["Wk"], D), by_group(att["Wv"], D)], axis=3)
        .reshape(KV, 2, 2, P, 2 * D).transpose(0, 1, 3, 2, 4).reshape(KV, 2, P, 4 * D),
        wo=att["Wo"].reshape(HID, KV, HG, D).transpose(1, 2, 3, 0),
        wlog=np.concatenate([att["Win"].T, ffn["router_w"], np.zeros((HID, P - LW), np.float32)], axis=1)
        .reshape(KC, P, P).transpose(1, 0, 2),
        dtb=att["dt_bias"], alog=att["A_log_bias"], gnw=att["gnorm_w"].reshape(D, 1),
        order=np.arange(E, 0, -1).astype(np.float32),
        rb=ffn["router_b"], rbias=ffn["router_bias"],
        w123=np.concatenate([up(ffn["ew1"], ffn["sw1"]), up(ffn["ew2"], ffn["sw2"]), w3], axis=2),
        b1=np.concatenate([ffn["eb1"], ffn["sb1"].reshape(2, P)]).T,
        b2=np.concatenate([ffn["eb2"], ffn["sb2"].reshape(2, P)]).T,
        b3=np.concatenate([ffn["eb3"], ffn["sb3"].reshape(1, HID)]),
        cos=np.concatenate([cos, cos]), sin=np.concatenate([-sin, sin]),
    )
    nc = bacc.Bacc("TRN2", target_bir_lowering=False, num_devices=1)
    feed, args = {}, {}
    for name, w in arrays.items():
        w = np.ascontiguousarray(w)
        feed[f"in_{name}"] = w
        args[name] = nc.dram_tensor(f"in_{name}", w.shape, mybir.dt.from_np(w.dtype), kind="ExternalInput").ap()
    args["gdram"] = nc.dram_tensor("decay_exponents", (HALVES, H, NT, P), F32, kind="Internal").ap()
    args["out"] = nc.dram_tensor("out", _OUT, F32, kind="ExternalOutput").ap()
    build(nc, **args)
    r = run_bass_kernel_spmd(nc, [feed], core_ids=[0])
    return np.asarray(r.results[0]["out"]).reshape(B, L, HID)
```
